# Optimizing a Trainium2 kernel written in Bass

```python
import numpy as np
import jax
import jax.numpy as jnp

def _softmax(x, axis=-1):
    return jax.nn.softmax(x, axis=axis)

def _gelu(x):
    return jax.nn.gelu(x, approximate=True)

def _silu(x):
    return jax.nn.silu(x)

def _sigmoid(x):
    return jax.nn.sigmoid(x)

def _layernorm(x, axis=-1, eps=1e-05):
    m = jnp.mean(x, axis=axis, keepdims=True)
    v = jnp.var(x, axis=axis, keepdims=True)
    return (x - m) / jnp.sqrt(v + eps)

def _scatter_add(tgt, idx, src, axis=0):
    return tgt.at[idx].add(src)

def _segment_sum(src, seg, n):
    return jax.ops.segment_sum(src, seg, n)
kernel_name = 'mk_perceiver_d2_seqx_r2_b13885'

def setup_inputs(seed: int=0):
    np.random.seed(seed)
    _w = jnp.asarray

    def _rec_inputs():
        import jax
        import jax.numpy as jnp
        _rk = jax.random.key(seed)
        x = -0.0002928 + 1 * jax.random.normal(jax.random.fold_in(_rk, 1), (32, 32, 512), jnp.float32)
        _lenS = 32 - jax.random.randint(jax.random.fold_in(_rk, 7), (32,), 0, max(1, 32 // 4) + 1, jnp.int32)
        _lenS2 = 257 - jax.random.randint(jax.random.fold_in(_rk, 8), (32,), 0, max(1, 257 // 4) + 1, jnp.int32)
        _ctx_1024P = jax.random.normal(jax.random.fold_in(_rk, 11), (32, 16, 512), jnp.float32)
        _ctx_1024c = jax.random.dirichlet(jax.random.fold_in(_rk, 511), 0.3 * jnp.ones((16,), jnp.float32), (32, 257))
        _ctx_1024t = jnp.einsum('bsk,bkd->bsd', _ctx_1024c, _ctx_1024P)
        _ctx_1024t = _ctx_1024t * jax.lax.rsqrt(jnp.mean(jnp.square(_ctx_1024t)) + 1e-12) * 0.953939
        ctx_1024 = -1.39393e-06 + 0.999914 * (_ctx_1024t + 0.3 * jax.random.normal(jax.random.fold_in(_rk, 611), (32, 257, 512), jnp.float32))
        _validS = jnp.arange(32)[None, :] < _lenS[:, None]
        _validS2 = jnp.arange(257)[None, :] < _lenS2[:, None]
        _causal = jnp.tril(jnp.ones((32, 32), dtype=bool))
        mask_BxS2_bf0 = jnp.logical_not(jnp.ones((32, 257), dtype=bool))
        return (x, ctx_1024, mask_BxS2_bf0)
    x, ctx_1024, mask_BxS2_bf0 = _rec_inputs()

    def _L0_xattn_setup():
        import jax, jax.numpy as jnp
        import numpy as np
        B, S, D = (2, 1024, 512)
        H, DK, DV = (16, 64, 64)
        NEG_INF = -1e+30
        key = jax.random.key(seed)
        ks = jax.random.split(key, 12)
        s = 0.02
        return {'queries': jax.random.normal(ks[0], (B, S, D), jnp.float32), 'keys': jax.random.normal(ks[1], (B, S, D), jnp.float32), 'values': jax.random.normal(ks[2], (B, S, D), jnp.float32), 'mask': jnp.zeros((B, S), dtype=bool), 'Wq': jax.random.normal(ks[3], (D, H * DK), jnp.float32) * s, 'bq': jnp.zeros((H * DK,), jnp.float32), 'Wk': jax.random.normal(ks[4], (D, H * DK), jnp.float32) * s, 'bk': jnp.zeros((H * DK,), jnp.float32), 'Wv': jax.random.normal(ks[5], (D, H * DV), jnp.float32) * s, 'bv': jnp.zeros((H * DV,), jnp.float32), 'Wo': jax.random.normal(ks[6], (H * DV, D), jnp.float32) * s, 'bo': jnp.zeros((D,), jnp.float32)}
    _L0_xattn_all = _L0_xattn_setup()
    _L0_xattn_in = {k: v for k, v in _L0_xattn_all.items() if k in ('Wq', 'bq', 'Wk', 'bk', 'Wv', 'bv', 'Wo', 'bo')}
    del _L0_xattn_all

    def _L0_attn_setup():
        import jax, jax.numpy as jnp
        import numpy as np
        N_HEADS = 16
        D_HEAD = 64
        WINDOW = 128
        NEG_INF = -jnp.inf
        key = jax.random.key(seed)
        k1, k2, k3, k4 = jax.random.split(key, 4)
        B, T, D = (2, 1024, 512)
        total = N_HEADS * D_HEAD
        x = jax.random.normal(k1, (B, T, D), dtype=jnp.float32)
        w_qkv = jax.random.normal(k2, (3 * total, D), dtype=jnp.float32) * (2.0 / (3 * total)) ** 0.5
        w_gate = jax.random.normal(k3, (total, D), dtype=jnp.float32) * (2.0 / total) ** 0.5
        w_out = jax.random.normal(k4, (D, total), dtype=jnp.float32) * (2.0 / D) ** 0.5
        return {'x': x, 'w_qkv': w_qkv, 'w_gate': w_gate, 'w_out': w_out}
    _L0_attn_all = _L0_attn_setup()
    _L0_attn_in = {k: v for k, v in _L0_attn_all.items() if k in ('w_qkv', 'w_gate', 'w_out')}
    del _L0_attn_all

    def _L0_ffn_setup():
        import jax, jax.numpy as jnp
        import numpy as np
        NUM_EXPERTS = 64
        TOP_K = 8
        HIDDEN = 512
        INTER = 384
        BATCH, SEQ = (1, 512)
        CAPACITY = 128

        def _moe_forward(hidden_states, gate_w, w_gate, w_up, w_down):
            B, S, H = hidden_states.shape
            x = hidden_states.reshape(-1, H)
            T = x.shape[0]
            logits = (x @ gate_w.T).astype(jnp.float32)
            probs = jax.nn.softmax(logits, axis=-1)
            topk_p, topk_i = jax.lax.top_k(probs, TOP_K)
            topk_p = topk_p / jnp.sum(topk_p, axis=-1, keepdims=True)
            flat_e = topk_i.reshape(-1)
            onehot = jax.nn.one_hot(flat_e, NUM_EXPERTS, dtype=jnp.int32)
            pos_all = jnp.cumsum(onehot, axis=0) - 1
            pos = jnp.take_along_axis(pos_all, flat_e[:, None], axis=1)[:, 0]
            x_rep = jnp.repeat(x, TOP_K, axis=0)
            dispatch = jnp.zeros((NUM_EXPERTS, CAPACITY, H), x.dtype)
            dispatch = dispatch.at[flat_e, pos].set(x_rep, mode='drop')
            g = jax.nn.silu(jnp.einsum('ech,eih->eci', dispatch, w_gate))
            u = jnp.einsum('ech,eih->eci', dispatch, w_up)
            y = jnp.einsum('eci,ehi->ech', g * u, w_down)
            valid = pos < CAPACITY
            y_tok = y[flat_e, jnp.minimum(pos, CAPACITY - 1)]
            w = (topk_p.reshape(-1) * valid.astype(topk_p.dtype)).astype(x.dtype)
            out = (y_tok * w[:, None]).reshape(T, TOP_K, H).sum(axis=1)
            return out.reshape(B, S, H)
        key = jax.random.key(seed)
        k1, k2, k3, k4, k5 = jax.random.split(key, 5)
        scale = 0.02
        return {'hidden_states': jax.random.normal(k1, (BATCH, SEQ, HIDDEN), dtype=jnp.float32), 'gate_w': jax.random.normal(k2, (NUM_EXPERTS, HIDDEN), dtype=jnp.float32) * scale, 'w_gate': jax.random.normal(k3, (NUM_EXPERTS, INTER, HIDDEN), dtype=jnp.float32) * scale, 'w_up': jax.random.normal(k4, (NUM_EXPERTS, INTER, HIDDEN), dtype=jnp.float32) * scale, 'w_down': jax.random.normal(k5, (NUM_EXPERTS, HIDDEN, INTER), dtype=jnp.float32) * scale}
    _L0_ffn_all = _L0_ffn_setup()
    _L0_ffn_in = {k: v for k, v in _L0_ffn_all.items() if k in ('gate_w', 'w_gate', 'w_up', 'w_down')}
    del _L0_ffn_all

    def _L1_xattn_setup():
        import jax, jax.numpy as jnp
        import numpy as np
        N, L, E, H, D = (4, 1024, 512, 16, 64)
        key = jax.random.key(seed)
        ks = jax.random.split(key, 8)
        s = 1.0 / np.sqrt(E)
        return {'Q': jax.random.normal(ks[0], (N, L, E), jnp.float32), 'K': jax.random.normal(ks[1], (N, L, E), jnp.float32), 'V': jax.random.normal(ks[2], (N, L, E), jnp.float32), 'Wq': jax.random.normal(ks[3], (H * D, E), jnp.float32) * s, 'bq': jnp.zeros((H * D,), jnp.float32), 'Wk': jax.random.normal(ks[4], (H * D, E), jnp.float32) * s, 'bk': jnp.zeros((H * D,), jnp.float32), 'Wv': jax.random.normal(ks[5], (H * D, E), jnp.float32) * s, 'bv': jnp.zeros((H * D,), jnp.float32), 'Wo': jax.random.normal(ks[6], (E, H * D), jnp.float32) * s, 'bo': jnp.zeros((E,), jnp.float32)}
    _L1_xattn_all = _L1_xattn_setup()
    _L1_xattn_in = {k: v for k, v in _L1_xattn_all.items() if k in ('Wq', 'bq', 'Wk', 'bk', 'Wv', 'bv', 'Wo', 'bo')}
    del _L1_xattn_all

    def _L1_attn_setup():
        import jax, jax.numpy as jnp
        import numpy as np
        N_HEADS = 16

        def _rope(t, sin, cos):
            t_rot = jnp.stack([-t[..., 1::2], t[..., ::2]], axis=-1).reshape(t.shape)
            return t * cos + t_rot * sin
        key = jax.random.key(seed)
        ks = jax.random.split(key, 5)
        B, S, D = (2, 1024, 512)
        scale = 1.0 / np.sqrt(D)
        return {'x': jax.random.normal(ks[0], (B, S, D), dtype=jnp.float32), 'Wq': jax.random.normal(ks[1], (D, D), dtype=jnp.float32) * scale, 'Wk': jax.random.normal(ks[2], (D, D), dtype=jnp.float32) * scale, 'Wv': jax.random.normal(ks[3], (D, D), dtype=jnp.float32) * scale, 'Wo': jax.random.normal(ks[4], (D, D), dtype=jnp.float32) * scale}
    _L1_attn_all = _L1_attn_setup()
    _L1_attn_in = {k: v for k, v in _L1_attn_all.items() if k in ('Wq', 'Wk', 'Wv', 'Wo')}
    del _L1_attn_all

    def _L1_ffn_setup():
        import jax, jax.numpy as jnp
        import numpy as np
        IN_F = 512
        OUT_F = 512
        N_EXPERTS = 8
        TOP_K = 2
        key = jax.random.key(seed)
        ks = jax.random.split(key, 5)
        scale_in = 1.0 / np.sqrt(IN_F)
        x = jax.random.normal(ks[0], (4, 1024, IN_F), dtype=jnp.float32)
        W_experts = jax.random.uniform(ks[1], (N_EXPERTS, OUT_F, IN_F), jnp.float32, -scale_in, scale_in)
        b_experts = jax.random.uniform(ks[2], (N_EXPERTS, OUT_F), jnp.float32, -scale_in, scale_in)
        W_router = jax.random.uniform(ks[3], (N_EXPERTS, IN_F), jnp.float32, -scale_in, scale_in)
        b_router = jax.random.uniform(ks[4], (N_EXPERTS,), jnp.float32, -scale_in, scale_in)
        return {'x': x, 'W_experts': W_experts, 'b_experts': b_experts, 'W_router': W_router, 'b_router': b_router}
    _L1_ffn_all = _L1_ffn_setup()
    _L1_ffn_in = {k: v for k, v in _L1_ffn_all.items() if k in ('W_experts', 'b_experts', 'W_router', 'b_router')}
    del _L1_ffn_all
    return {'x': x, 'ctx_1024': ctx_1024, 'mask_BxS2_bf0': mask_BxS2_bf0, 'L0_xattn_Wq': _L0_xattn_in['Wq'], 'L0_xattn_bq': _L0_xattn_in['bq'], 'L0_xattn_Wk': _L0_xattn_in['Wk'], 'L0_xattn_bk': _L0_xattn_in['bk'], 'L0_xattn_Wv': _L0_xattn_in['Wv'], 'L0_xattn_bv': _L0_xattn_in['bv'], 'L0_xattn_Wo': _L0_xattn_in['Wo'], 'L0_xattn_bo': _L0_xattn_in['bo'], 'L0_attn_w_qkv': _L0_attn_in['w_qkv'], 'L0_attn_w_gate': _L0_attn_in['w_gate'], 'L0_attn_w_out': _L0_attn_in['w_out'], 'L0_ffn_gate_w': _L0_ffn_in['gate_w'], 'L0_ffn_w_gate': _L0_ffn_in['w_gate'], 'L0_ffn_w_up': _L0_ffn_in['w_up'], 'L0_ffn_w_down': _L0_ffn_in['w_down'], 'L1_xattn_Wq': _L1_xattn_in['Wq'], 'L1_xattn_bq': _L1_xattn_in['bq'], 'L1_xattn_Wk': _L1_xattn_in['Wk'], 'L1_xattn_bk': _L1_xattn_in['bk'], 'L1_xattn_Wv': _L1_xattn_in['Wv'], 'L1_xattn_bv': _L1_xattn_in['bv'], 'L1_xattn_Wo': _L1_xattn_in['Wo'], 'L1_xattn_bo': _L1_xattn_in['bo'], 'L1_attn_Wq': _L1_attn_in['Wq'], 'L1_attn_Wk': _L1_attn_in['Wk'], 'L1_attn_Wv': _L1_attn_in['Wv'], 'L1_attn_Wo': _L1_attn_in['Wo'], 'L1_ffn_W_experts': _L1_ffn_in['W_experts'], 'L1_ffn_b_experts': _L1_ffn_in['b_experts'], 'L1_ffn_W_router': _L1_ffn_in['W_router'], 'L1_ffn_b_router': _L1_ffn_in['b_router']}

def reference(x, ctx_1024, mask_BxS2_bf0, L0_xattn_Wq, L0_xattn_bq, L0_xattn_Wk, L0_xattn_bk, L0_xattn_Wv, L0_xattn_bv, L0_xattn_Wo, L0_xattn_bo, L0_attn_w_qkv, L0_attn_w_gate, L0_attn_w_out, L0_ffn_gate_w, L0_ffn_w_gate, L0_ffn_w_up, L0_ffn_w_down, L1_xattn_Wq, L1_xattn_bq, L1_xattn_Wk, L1_xattn_bk, L1_xattn_Wv, L1_xattn_bv, L1_xattn_Wo, L1_xattn_bo, L1_attn_Wq, L1_attn_Wk, L1_attn_Wv, L1_attn_Wo, L1_ffn_W_experts, L1_ffn_b_experts, L1_ffn_W_router, L1_ffn_b_router):
    import jax
    import jax.numpy as jnp

    def _L0_xattn_ref(queries, keys, values, mask, Wq, bq, Wk, bk, Wv, bv, Wo, bo):
        import jax, jax.numpy as jnp
        import numpy as np
        B, S, D = (2, 1024, 512)
        H, DK, DV = (16, 64, 64)
        NEG_INF = -1e+30
        b, sq, _ = queries.shape
        sk = keys.shape[1]
        q = (queries @ Wq + bq).reshape(b, sq, H, DK).transpose(0, 2, 1, 3)
        k = (keys @ Wk + bk).reshape(b, sk, H, DK).transpose(0, 2, 1, 3)
        v = (values @ Wv + bv).reshape(b, sk, H, DV).transpose(0, 2, 1, 3)
        scores = jnp.einsum('bhqd,bhkd->bhqk', q, k) / jnp.sqrt(jnp.float32(DK))
        scores = jnp.where(mask[:, None, None, :], NEG_INF, scores)
        causal = jnp.triu(jnp.ones((sq, sk), dtype=bool), k=1)
        scores = jnp.where(causal[None, None], NEG_INF, scores)
        attn = jax.nn.softmax(scores, axis=-1)
        out = jnp.einsum('bhqk,bhkd->bhqd', attn, v)
        out = out.transpose(0, 2, 1, 3).reshape(b, sq, H * DV)
        return out @ Wo + bo

    def _L0_attn_ref(x, w_qkv, w_gate, w_out):
        import jax, jax.numpy as jnp
        import numpy as np
        N_HEADS = 16
        D_HEAD = 64
        WINDOW = 128
        NEG_INF = -jnp.inf
        B, T, D = x.shape
        H, Dh = (N_HEADS, D_HEAD)
        scale = Dh ** (-0.5)
        qkv = x @ w_qkv.T
        q, k, v = jnp.split(qkv, 3, axis=-1)
        q = q.reshape(B, T, H, Dh).transpose(0, 2, 1, 3)
        k = k.reshape(B, T, H, Dh).transpose(0, 2, 1, 3)
        v = v.reshape(B, T, H, Dh).transpose(0, 2, 1, 3)
        scores = jnp.einsum('bhqd,bhkd->bhqk', q, k) * scale
        pos = jnp.arange(T)
        dist = pos[:, None] - pos[None, :]
        valid = (dist >= 0) & (dist < WINDOW)
        scores = jnp.where(valid[None, None], scores, NEG_INF)
        attn = jax.nn.softmax(scores, axis=-1)
        out = jnp.einsum('bhqk,bhkd->bhqd', attn, v)
        out = out.transpose(0, 2, 1, 3).reshape(B, T, H * Dh)
        gate = jax.nn.sigmoid(x @ w_gate.T)
        return out * gate @ w_out.T

    def _L0_ffn_ref(hidden_states, gate_w, w_gate, w_up, w_down):
        import jax, jax.numpy as jnp
        import numpy as np
        NUM_EXPERTS = 64
        TOP_K = 8
        HIDDEN = 512
        INTER = 384
        BATCH, SEQ = (1, 512)
        CAPACITY = 128

        def _moe_forward(hidden_states, gate_w, w_gate, w_up, w_down):
            B, S, H = hidden_states.shape
            x = hidden_states.reshape(-1, H)
            T = x.shape[0]
            logits = (x @ gate_w.T).astype(jnp.float32)
            probs = jax.nn.softmax(logits, axis=-1)
            topk_p, topk_i = jax.lax.top_k(probs, TOP_K)
            topk_p = topk_p / jnp.sum(topk_p, axis=-1, keepdims=True)
            flat_e = topk_i.reshape(-1)
            onehot = jax.nn.one_hot(flat_e, NUM_EXPERTS, dtype=jnp.int32)
            pos_all = jnp.cumsum(onehot, axis=0) - 1
            pos = jnp.take_along_axis(pos_all, flat_e[:, None], axis=1)[:, 0]
            x_rep = jnp.repeat(x, TOP_K, axis=0)
            dispatch = jnp.zeros((NUM_EXPERTS, CAPACITY, H), x.dtype)
            dispatch = dispatch.at[flat_e, pos].set(x_rep, mode='drop')
            g = jax.nn.silu(jnp.einsum('ech,eih->eci', dispatch, w_gate))
            u = jnp.einsum('ech,eih->eci', dispatch, w_up)
            y = jnp.einsum('eci,ehi->ech', g * u, w_down)
            valid = pos < CAPACITY
            y_tok = y[flat_e, jnp.minimum(pos, CAPACITY - 1)]
            w = (topk_p.reshape(-1) * valid.astype(topk_p.dtype)).astype(x.dtype)
            out = (y_tok * w[:, None]).reshape(T, TOP_K, H).sum(axis=1)
            return out.reshape(B, S, H)
        return _moe_forward(hidden_states, gate_w, w_gate, w_up, w_down)

    def _L1_xattn_ref(Q, K, V, Wq, bq, Wk, bk, Wv, bv, Wo, bo):
        import jax, jax.numpy as jnp
        import numpy as np
        N, L, E, H, D = (4, 1024, 512, 16, 64)
        n, lq, e = Q.shape
        lk = K.shape[1]
        q = (Q @ Wq.T + bq).reshape(n, lq, H, D)
        k = (K @ Wk.T + bk).reshape(n, lk, H, D)
        v = (V @ Wv.T + bv).reshape(n, lk, H, D)
        scores = jnp.einsum('nqhd,nkhd->nqkh', q, k) / jnp.sqrt(jnp.float32(D))
        attn = jax.nn.softmax(scores, axis=2)
        out = jnp.einsum('nqkh,nkhd->nqhd', attn, v)
        out = out.reshape(n, lq, H * D)
        return (out @ Wo.T + bo).reshape(n, lq, E)

    def _L1_attn_ref(x, Wq, Wk, Wv, Wo):
        import jax, jax.numpy as jnp
        import numpy as np
        N_HEADS = 16

        def _rope(t, sin, cos):
            t_rot = jnp.stack([-t[..., 1::2], t[..., ::2]], axis=-1).reshape(t.shape)
            return t * cos + t_rot * sin
        B, S, D = x.shape
        H = N_HEADS
        dk = D // H
        q = (x @ Wq.T).reshape(B, S, H, dk).transpose(0, 2, 1, 3)
        k = (x @ Wk.T).reshape(B, S, H, dk).transpose(0, 2, 1, 3)
        v = (x @ Wv.T).reshape(B, S, H, dk).transpose(0, 2, 1, 3)
        inv_freq = 1.0 / 10000.0 ** (jnp.arange(0, dk, 2, dtype=jnp.float32) / dk)
        pos = jnp.arange(S, dtype=jnp.float32)
        freqs = pos[:, None] * inv_freq[None, :]
        sin = jnp.repeat(jnp.sin(freqs), 2, axis=-1)
        cos = jnp.repeat(jnp.cos(freqs), 2, axis=-1)
        q = _rope(q, sin, cos)
        k = _rope(k, sin, cos)
        scores = jnp.einsum('bhqd,bhkd->bhqk', q, k) / jnp.sqrt(jnp.float32(dk))
        slopes = 2.0 ** (-8.0 * jnp.arange(H, dtype=jnp.float32) / H)
        rel = -jnp.abs(pos[:, None] - pos[None, :])
        scores = scores + slopes[None, :, None, None] * rel[None, None]
        attn = jax.nn.softmax(scores, axis=-1)
        out = jnp.einsum('bhqk,bhkd->bhqd', attn, v)
        out = out.transpose(0, 2, 1, 3).reshape(B, S, D)
        return out @ Wo.T

    def _L1_ffn_ref(x, W_experts, b_experts, W_router, b_router):
        import jax, jax.numpy as jnp
        import numpy as np
        IN_F = 512
        OUT_F = 512
        N_EXPERTS = 8
        TOP_K = 2
        router_logits = jnp.einsum('bsd,ed->bse', x, W_router) + b_router
        router_weights = jax.nn.softmax(router_logits, axis=-1)
        if TOP_K < N_EXPERTS:
            topk_w, topk_idx = jax.lax.top_k(router_weights, TOP_K)
            sparse = jnp.zeros_like(router_weights)
            router_weights = jnp.take_along_axis(sparse, topk_idx, axis=-1)
            router_weights = sparse.at[..., :].set(0.0)
            b_idx = jnp.arange(sparse.shape[0])[:, None, None]
            s_idx = jnp.arange(sparse.shape[1])[None, :, None]
            router_weights = sparse.at[b_idx, s_idx, topk_idx].set(topk_w)
        expert_out = jnp.einsum('bsd,eod->bseo', x, W_experts) + b_experts
        return jnp.einsum('bseo,bse->bso', expert_out, router_weights)
    x = x + _L0_xattn_ref(_layernorm(x, axis=-1), ctx_1024, ctx_1024, mask_BxS2_bf0, L0_xattn_Wq, L0_xattn_bq, L0_xattn_Wk, L0_xattn_bk, L0_xattn_Wv, L0_xattn_bv, L0_xattn_Wo, L0_xattn_bo)
    x = x + _L0_attn_ref(_layernorm(x, axis=-1), L0_attn_w_qkv, L0_attn_w_gate, L0_attn_w_out)
    x = x + _L0_ffn_ref(_layernorm(x, axis=-1), L0_ffn_gate_w, L0_ffn_w_gate, L0_ffn_w_up, L0_ffn_w_down)
    x = x + _L1_xattn_ref(_layernorm(x, axis=-1), ctx_1024, ctx_1024, L1_xattn_Wq, L1_xattn_bq, L1_xattn_Wk, L1_xattn_bk, L1_xattn_Wv, L1_xattn_bv, L1_xattn_Wo, L1_xattn_bo)
    x = x + _L1_attn_ref(_layernorm(x, axis=-1), L1_attn_Wq, L1_attn_Wk, L1_attn_Wv, L1_attn_Wo)
    x = x + _L1_ffn_ref(_layernorm(x, axis=-1), L1_ffn_W_experts, L1_ffn_b_experts, L1_ffn_W_router, L1_ffn_b_router)
    return x

_drawn_inputs = setup_inputs


def setup_inputs(seed=0):
    import zlib

    import numpy as np

    out = dict(_drawn_inputs(seed))
    spreads = {'L0_xattn_bq': (0.0, 0.8),
     'L0_xattn_bk': (0.0, 0.8),
     'L0_xattn_bv': (0.0, 0.1),
     'L0_xattn_bo': (0.0, 0.1),
     'L1_xattn_bq': (0.0, 0.271),
     'L1_xattn_bk': (0.0, 0.8),
     'L1_xattn_bv': (0.0, 0.1),
     'L1_xattn_bo': (0.0, 0.1)}
    factors = {'L0_xattn_Wq': 3.626,
     'L0_xattn_Wk': 3.55,
     'L0_ffn_gate_w': 3.785,
     'L0_ffn_w_gate': 3.434,
     'L0_ffn_w_up': 3.291,
     'L0_ffn_w_down': 3.38,
     'L1_ffn_b_experts': 8.0,
     'L1_ffn_b_router': 2.675}
    for name, (base, spread) in spreads.items():
        noise = np.random.default_rng([zlib.crc32(name.encode()), seed]).standard_normal(out[name].shape)
        drawn = base * np.exp(spread * noise) if base else spread * noise
        out[name] = jnp.asarray(drawn.astype(out[name].dtype))
    for name, factor in factors.items():
        out[name] = (out[name] * factor).astype(out[name].dtype)
    return out
```

```python
from contextlib import ExitStack, contextmanager

import concourse.bass as bass
from concourse import mybir

F32 = mybir.dt.float32
BF16 = mybir.dt.bfloat16
I32 = mybir.dt.int32
U32 = mybir.dt.uint32
U8 = mybir.dt.uint8
ALU = mybir.AluOpType
ACT = mybir.ActivationFunctionType
AX = mybir.AxisListType

P = 128
B, S, D = 32, 32, 512
TILES = B * S // P
SEQS = P // S
KD = D // P
NCTX = 257
TAIL = NCTX - S
H = 16
DH = 64
HD = H * DH
BANK = 512
EXPERTS, TOPK, CAP, INTER = 64, 8, 128, 384
EXPERTS1, TOPK1 = 8, 2
SLOTS = 4
EW = KD * INTER * 2 + INTER // P * D
MASKED = -1e30
APART = -3e38
EPS = 1e-5
INFO = 6
NOWHERE = 4096
UNSEEN = 1024


class Count:

    def __init__(self):
        self.n, self.i, self.per = 0, None, 0

    def add(self, k=1):
        self.n += k

    def value(self, back=0):
        n = self.n - back
        return n if self.i is None else self.i * self.per + n


@contextmanager
def rounds(eng, n, per):
    starts = [c.n for c, _ in per]
    with eng.Fori(0, n) as i:
        for c, k in per:
            c.i, c.per = i, k
        yield i
    for (c, k), start in zip(per, starts):
        assert c.n == start + k, (c.n - start, k)
        c.i, c.per, c.n = None, 0, start + k * n


def wait(eng, sem, value):
    if not isinstance(value, int) or value > 0:
        eng.wait_ge(sem, value)


class Counts:

    def __init__(self):
        self.xn, self.proj, self.tp, self.p, self.sm = Count(), Count(), Count(), Count(), Count()
        self.s, self.o, self.rest, self.ctxh, self.tail = Count(), Count(), Count(), Count(), Count()
        self.gate, self.sel, self.norm, self.wmat, self.route = Count(), Count(), Count(), Count(), Count()
        self.ctx = [Count(), Count()]


class Attention:

    def __init__(self, name, dh, loads, cross=False, gated=False, rope=False):
        self.name, self.dh, self.loads = name, dh, loads
        self.cross, self.gated, self.rope = cross, gated, rope
        self.width = H * dh
        self.halves = self.width // BANK
        self.chunks = self.width // P
        self.parts = 3 - self.halves
        self.early = [(w, h) for w in "qk" for h in range(self.halves)]
        kinds = ["v"] + ["rest"] * cross + ["gate"] * gated
        self.late = [(w, h) for w in kinds for h in range(self.halves)]
        self.rows = P // dh
        self.places = [c * self.rows + r for r in range(self.rows) for c in range(H // self.rows)]
        self.order = [0, 2, 1, 3] if self.rows == 2 else [0, 1, 2, 3]
        self.per_proj = self.parts + len(self.early) + len(self.late) + 1
        self.per_tp = 4 + 2 * self.halves + 2


def build(nc, t):
    with ExitStack() as ctx:
        def sb(name, words, dt=F32):
            return ctx.enter_context(nc.sbuf_tensor(name, [P, words], dt))[:, :]

        def sem(name):
            return ctx.enter_context(nc.semaphore(name))

        def carve(buf, base, *sizes):
            for n in sizes:
                assert base + n <= buf.shape[1], (base, n)
                yield buf[:, base:base + n]
                base += n

        x = sb("x", TILES * D)
        arena = sb("arena", 33280)
        work = sb("work", 14464)
        small = sb("small", 1240)
        ident = sb("ident", P)
        psum = ctx.enter_context(nc.psum_tensor("psum", [P, 8 * BANK], F32))[:, :]
        bank = [psum[:, n * BANK:(n + 1) * BANK] for n in range(8)]
        PROJ, SCORE, TP = 0, 2, 6

        W = KD * HD
        wq0, wk0, wv0, wo0 = carve(arena, 0, W, W, W, W)
        wgate0, wout0 = carve(arena, 0, W, W)
        wqkv0, bq0, bk0, bv0, bo0 = carve(arena, 17408, 3 * W, HD, HD, HD, D)
        slots = list(carve(arena, 2 * W, *[EW] * SLOTS))
        wk1, wv1, qp, ut = carve(arena, 0, W, W, KD * H * P, KD * H * P)
        wo1, wq1, bo1 = carve(arena, 24576, W, W, D)
        W1 = KD * D
        rope, alibi = carve(arena, 0, 4 * D, H * P)
        awv1, awo1, awq1, awk1 = carve(arena, 24576, W1, W1, W1, W1)
        (wexp1,) = carve(arena, 2 * W, EXPERTS1 * W1)

        xn, xnT = carve(work, 0, D, D)
        (ctxh, q, k, v, gate, qT, kT, s, pT, tail, rest) = carve(
            work, 2 * D, D, HD, HD, HD, HD, HD, HD, H * P, H * P, KD * TAIL, D)
        o, oT = s[:, 0:HD], pT[:, 0:HD]
        vrest = gate

        (router0, logit, prob, sel, ranked, chosen, wsel, wrest, eq, selb, cumb, posm, slotinfo, iota64, iota128,
         tokens, tri, ones, onehot0, onehot1, xg0, xg1, xgT0, xgT1, gexp, hid, hidT, y0, y1) = carve(
            work, 2 * D, KD * EXPERTS, EXPERTS, EXPERTS, EXPERTS, TOPK, TOPK, EXPERTS, EXPERTS, TOPK * EXPERTS,
            EXPERTS // 2, EXPERTS // 2, TILES * EXPERTS, TILES * EXPERTS * INFO // 2, EXPERTS, CAP,
            TILES * 3, P // 2, P // 2, TILES * CAP // 2, TILES * CAP // 2, D, D, D, D, INTER, INTER, INTER, D, D)
        chosen_u = chosen.bitcast(U32)
        selb, cumb, slotinfo, tri, ones = (b.bitcast(BF16) for b in (selb, cumb, slotinfo, tri, ones))
        onehot, xg, xgT, y = [onehot0.bitcast(BF16), onehot1.bitcast(BF16)], [xg0, xg1], [xgT0, xgT1], [y0, y1]

        (q1, qT1, p1, pT1, u0, u1, ctxT0, ctxr0, ctxl0, ctxT1, ctxr1, ctxl1, bq1, bk1, bv1) = carve(
            work, 2 * D, HD, HD, SEQS * NCTX, 2 * SEQS * P, D, D, *[KD * NCTX, 2 * D, D] * 2, HD, HD, HD)
        u, uu = [u0, u1], work[:, 2 * D + 2 * HD + SEQS * NCTX + 2 * SEQS * P:][:, 0:2 * D]
        ctxT, ctxr, ctxl = [ctxT0, ctxT1], [ctxr0, ctxr1], [ctxl0, ctxl1]
        o1, oT1 = q1, qT1

        router1, wmat, wT, bexp, brouter, iota8, logit1, prob1, pick, ranked1, chosen1 = carve(
            work, 2 * D, KD * EXPERTS1, P, P, D, *[EXPERTS1] * 7)

        def some(n, at=[0]):
            at[0] += n
            assert at[0] <= 1240, at
            return small[:, at[0] - n:at[0]]

        stats, mv, var, half, root, step = some(6), some(2), some(1), some(1), some(1), some(1)
        negmax, total, inv, restp = some(H), some(H), some(H), some(H)
        blockmask, causal, apart = some(P), some(P), some(P)
        keymask = some(TILES * S)
        keymask_u8 = some(TILES * S // 4)
        csum = some(KD * SEQS)
        top, rsum, rinv = some(1), some(1), some(1)
        gidx, sidx, wslot = some(SLOTS), some(SLOTS), some(SLOTS)
        fidx, empty, zero, held = some(1), some(1), some(1), some(1)
        ctok, crow, negc, total1 = some(H), some(H), some(SEQS), some(SEQS)
        plast = restp[:, 0:SEQS]

        xn_d = nc.dram_tensor("xn_rows", (B * S, D), F32, kind="Internal").ap()
        x_d = nc.dram_tensor("x_rows", (B * S, D), F32, kind="Internal").ap()

        s_x, s_const = sem("x_loaded"), sem("constants_loaded")
        s_w = {n: sem("loaded_" + n) for n in ("q0", "k0", "v0", "o0", "bias0", "qkv0", "gate0", "out0", "tables0",
                                         "k1", "v1", "q1", "o1", "bias1", "bo1", "rope", "alibi", "aq1", "ak1", "av1", "ao1",
                                         "tables1", "experts1")}
        s_ctxh, s_tail, s_tail_used = sem("ctx_head_loaded"), sem("ctx_tail_loaded"), sem("ctx_tail_summed")
        s_rest = sem("ctx_rest_ready")
        s_ready = sem("small_tables_ready")
        s_xn = sem("xn_ready")
        s_proj, s_proj_free = sem("projection_full"), sem("projection_taken")
        s_tp, s_tp_free = sem("transposed_full"), sem("transposed_taken")
        s_s, s_sm, s_p = sem("scores_full"), sem("scores_masked"), sem("probs_ready")
        s_o, s_o_ready = sem("output_full"), sem("output_ready")
        s_gate, s_gate_exp = sem("gate_negated"), sem("gate_exp_ready")
        s_end = {n: sem("finished_" + n) for n in ("xattn0", "attn0", "moe0", "xattn1", "attn1")}
        s_out = sem("stored")
        s_xn_d, s_x_d, s_x_back = sem("xn_rows_written"), sem("x_rows_written"), [sem("x_tile0_back"), sem("x_back")]
        s_logit, s_exp, s_sel = sem("logits_ready"), sem("routing_exp_ready"), sem("choice_ready")
        s_ew = [sem(f"expert_weights_{j}") for j in range(SLOTS)]
        s_onehot, s_idx, s_slot = sem("onehot_ready"), sem("slots_full"), sem("slots_ready")
        s_gather = [sem("gathered_even"), sem("gathered_odd")]
        s_xgt, s_xgt_free = sem("slots_turned"), sem("slots_turned_taken")
        s_g, s_gu, s_gexp, s_h = sem("gate_full"), sem("up_full"), sem("expert_exp_ready"), sem("hidden_ready")
        s_ht, s_ht_free, s_y, s_y_ready = sem("hidden_turned"), sem("hidden_turned_taken"), sem("down_full"), sem("down_ready")
        s_scatter = sem("scattered")
        s_ctx = [sem("ctx_even_loaded"), sem("ctx_odd_loaded")]
        s_norm, s_q1 = sem("probs_normalised"), sem("q_ready")
        s_held = sem("held")
        s_wmat, s_final = sem("expert_shares_ready"), sem("tile_final")

        xattn0 = Attention("xattn0", DH, ("q0", "k0", "v0", "o0"), cross=True)
        attn0 = Attention("attn0", DH, ("qkv0", "gate0", "out0"), gated=True)
        attn1 = Attention("attn1", D // H, ("rope", "alibi", "aq1", "ak1", "av1", "ao1"), rope=True)
        weights = {(attn1, "q"): awq1, (attn1, "k"): awk1, (attn1, "v"): awv1, (attn1, "out"): awo1, (xattn0, "q"): wq0, (xattn0, "k"): wk0, (xattn0, "v"): wv0, (xattn0, "rest"): wv0,
                   (xattn0, "out"): wo0, (attn0, "gate"): wgate0, (attn0, "out"): wout0}
        for n, which in enumerate("qkv"):
            weights[attn0, which] = wqkv0[:, n * W:(n + 1) * W]

        def moving(st, which, half_):
            w = weights[st, which].rearrange("p (k n) -> p k n", k=KD)
            return w[:, :, half_ * BANK:(half_ + 1) * BANK]

        block = ctx.enter_context(nc.Block())

        ROUTE_PROJ, CROSS_PROJ = 4, 3 + H
        CROSS_TILE = CROSS_PROJ + SEQS * 4 + 3

        def pe_project(pe, c, emit, banks=2):
            wait(pe, s_proj_free, c.proj.value(banks - 1))
            emit(bank[PROJ + c.proj.n % banks]).then_inc(s_proj, 1)
            c.proj.add()

        def pe_transpose(pe, c, pieces):
            wait(pe, s_tp_free, c.tp.value(1))
            to = bank[TP + c.tp.n % 2]
            for j, src in enumerate(pieces):
                done = nc.tensor.transpose(to[:, j * P:(j + 1) * P], src, ident[:, :])
            done.then_inc(s_tp, 1)
            c.tp.add()

        def pe_turn_xn(pe, c, parts, banks=2):
            c.xn.add()
            wait(pe, s_xn, c.xn.value())
            n = KD // parts
            for part in range(parts):
                def emit(to):
                    for j in range(n):
                        at = (part * n + j) * P
                        done = nc.tensor.transpose(to[:, j * P:(j + 1) * P], xn[:, at:at + P], ident[:, :])
                    return done
                pe_project(pe, c, emit, banks)

        def attention_pe(pe, st, c):
            def projections(blocks):
                for which, half_ in blocks:
                    src = xnT
                    if st.cross and which in "kv":
                        src = ctxh
                    if st.cross and which == "k" and half_ == 0:
                        c.ctxh.add(16)
                        wait(pe, s_ctxh, c.ctxh.value())
                    if which == "rest":
                        src = rest
                        if half_ == 0:
                            c.rest.add()
                            wait(pe, s_rest, c.rest.value())
                    w = moving(st, which, half_)

                    def emit(to):
                        for j in range(KD):
                            done = nc.tensor.matmul(to, src[:, j * P:(j + 1) * P], w[:, j, :],
                                                    start=(j == 0), stop=(j == KD - 1))
                        return done
                    pe_project(pe, c, emit)

            def first_half():
                pe_turn_xn(pe, c, st.parts)
                wait(pe, s_proj_free, c.proj.value())
                projections(st.early)

            def turn_qk():
                wait(pe, s_proj_free, c.proj.value(len(st.late)))
                for src in (q, k):
                    for half_ in range(st.halves):
                        pe_transpose(pe, c, [src[:, (half_ * 4 + j) * P:(half_ * 4 + j + 1) * P] for j in range(4)])
                return c.tp.value()

            def scores(turned):
                wait(pe, s_tp_free, turned)
                for h in range(H):
                    ch, off = divmod(h * st.dh, P)
                    n = st.places.index(h)
                    done = nc.tensor.matmul(bank[SCORE + n // 4][:, n % 4 * P:(n % 4 + 1) * P],
                                            qT[off:off + st.dh, ch * P:(ch + 1) * P],
                                            kT[off:off + st.dh, ch * P:(ch + 1) * P], start=True, stop=True)
                    if n % 4 == 3:
                        done.then_inc(s_s, 1)

            def turn_probs():
                for g in st.order:
                    c.p.add()
                    wait(pe, s_p, c.p.value())
                    pe_transpose(pe, c, [s[:, (4 * g + j) * P:(4 * g + j + 1) * P] for j in range(4)])

            def values():
                for m, g in enumerate(st.order):
                    wait(pe, s_tp_free, c.tp.value(3 - m))
                    for n in range(4 * g, 4 * g + 4):
                        at = st.places[n] * st.dh
                        done = nc.tensor.matmul(bank[SCORE + at // BANK][:, at % BANK:at % BANK + st.dh],
                                                pT[:, n * P:(n + 1) * P], v[:, at:at + st.dh], start=True, stop=True)
                done.then_inc(s_o, 1)

            def turn_out():
                c.o.add()
                wait(pe, s_o_ready, c.o.value())
                n = st.chunks // 2
                for part in range(2):
                    pe_transpose(pe, c, [o[:, (part * n + j) * P:(part * n + j + 1) * P] for j in range(n)])

            def project_out():
                wait(pe, s_tp_free, c.tp.value())
                w = weights[st, "out"].rearrange("p (k n) -> p k n", k=st.chunks)

                def emit(to):
                    for j in range(st.chunks):
                        done = nc.tensor.matmul(to, oT[:, j * P:(j + 1) * P], w[:, j, :],
                                                start=(j == 0), stop=(j == st.chunks - 1))
                    return done
                pe_project(pe, c, emit)

            for name in st.loads:
                pe.wait_ge(s_w[name], 16)
            first_half()
            wait(pe, s_proj_free, c.proj.value(1))
            projections(st.late)
            scores(turn_qk())
            counts = [(c.xn, 1), (c.proj, st.per_proj), (c.tp, st.per_tp), (c.p, 4), (c.o, 1)]
            if st.cross:
                counts += [(c.ctxh, 16), (c.rest, 1)]
            with rounds(pe, TILES - 1, counts):
                first_half()
                turn_probs()
                values()
                projections(st.late)
                turned = turn_qk()
                turn_out()
                scores(turned)
                project_out()
            turn_probs()
            values()
            turn_out()
            project_out()

        def route_pe(pe, c):
            def tile():
                pe_turn_xn(pe, c, 2)
                wait(pe, s_proj_free, c.proj.value())

                def logits(to):
                    for j in range(KD):
                        done = nc.tensor.matmul(to[:, 0:EXPERTS], xnT[:, j * P:(j + 1) * P],
                                                router0[:, j * EXPERTS:(j + 1) * EXPERTS], start=(j == 0), stop=(j == KD - 1))
                    return done

                def positions(to):
                    nc.tensor.matmul(to[:, 0:EXPERTS], tri, selb, start=True, stop=False)
                    return nc.tensor.matmul(to[:, 0:EXPERTS], ones, cumb, start=False, stop=True)
                pe_project(pe, c, logits)
                c.sel.add()
                wait(pe, s_sel, c.sel.value())
                pe_project(pe, c, positions)

            pe.wait_ge(s_w["tables0"], 16 * TABLES0)
            tile()
            with rounds(pe, TILES - 1, [(c.xn, 1), (c.proj, ROUTE_PROJ), (c.sel, 1)]):
                tile()

        def experts_pe(pe, c):
            def slots_of(e, r):
                wait(pe, s_onehot, 4 * r + e + 1)
                wait(pe, s_slot, 4 * r + e)
                info = slotinfo.rearrange("p (t e n) -> p t e n", t=TILES, e=EXPERTS)
                for j in range(TILES):
                    at = 4 * r + e
                    if isinstance(at, int):
                        rhs = info[:, j, at, :]
                    else:
                        rhs = slotinfo[:, bass.ds(at * INFO + j * EXPERTS * INFO, INFO)]
                    done = nc.tensor.matmul(bank[7][:, 0:INFO], onehot[e % 2][:, j * CAP:(j + 1) * CAP], rhs,
                                            start=(j == 0), stop=(j == TILES - 1))
                done.then_inc(s_idx, 1)

            def turn(e, r):
                wait(pe, s_gather[e % 2], 32 * r + 16 * (e // 2) + 16)
                wait(pe, s_xgt_free, 4 * r + e)
                for j in range(KD):
                    done = nc.tensor.transpose(bank[4][:, j * P:(j + 1) * P], xg[e % 2][:, j * P:(j + 1) * P], ident)
                done.then_inc(s_xgt, 1)

            def gate_up(e, r):
                wait(pe, s_ew[e % SLOTS], 16 * r + 16 * (e // SLOTS) + 16)
                wait(pe, s_xgt_free, 4 * r + e + 1)
                for m in range(2):
                    w = slots[e % SLOTS][:, m * KD * INTER:(m + 1) * KD * INTER]
                    for j in range(KD):
                        done = nc.tensor.matmul(bank[e % 2 * 2 + m][:, 0:INTER], xgT[e % 2][:, j * P:(j + 1) * P],
                                                w[:, j * INTER:(j + 1) * INTER], start=(j == 0), stop=(j == KD - 1))
                    done.then_inc([s_g, s_gu][m], 1)

            def down(e, r):
                wait(pe, s_h, 4 * r + e + 1)
                for j in range(INTER // P):
                    done = nc.tensor.transpose(bank[5][:, j * P:(j + 1) * P], hid[:, j * P:(j + 1) * P], ident)
                done.then_inc(s_ht, 1)
                wait(pe, s_ht_free, 4 * r + e + 1)
                w = slots[e % SLOTS][:, 2 * KD * INTER:]
                for j in range(INTER // P):
                    done = nc.tensor.matmul(bank[6], hidT[:, j * P:(j + 1) * P], w[:, j * D:(j + 1) * D],
                                            start=(j == 0), stop=(j == INTER // P - 1))
                done.then_inc(s_y, 1)

            for e in range(3):
                slots_of(e, 0)
            turn(0, 0)
            gate_up(0, 0)

            def four(r, final):
                for e in range(SLOTS):
                    if not (final and e == 3):
                        turn(e + 1, r)
                        gate_up(e + 1, r)
                    if not (final and e >= 1):
                        slots_of(e + 3, r)
                    down(e, r)
            with pe.Fori(0, EXPERTS // SLOTS - 1) as r:
                four(r, False)
            four(EXPERTS // SLOTS - 1, True)

        def cross_pe(pe, c):
            qpv = qp.rearrange("p (c b n) -> p c b n", c=KD, b=SEQS)
            utv = ut.rearrange("p (c h n) -> p c h n", c=KD, h=H)

            def queries():
                pe_turn_xn(pe, c, 1)
                wait(pe, s_proj_free, c.proj.value())
                w = wq1.rearrange("p (k n) -> p k n", k=KD)
                for half_ in range(2):
                    def emit(to):
                        for j in range(KD):
                            done = nc.tensor.matmul(to, xnT[:, j * P:(j + 1) * P], w[:, j, half_ * BANK:(half_ + 1) * BANK],
                                                    start=(j == 0), stop=(j == KD - 1))
                        return done
                    pe_project(pe, c, emit)
                wait(pe, s_proj_free, c.proj.value())
                for half_ in range(2):
                    pe_transpose(pe, c, [q1[:, (half_ * 4 + j) * P:(half_ * 4 + j + 1) * P] for j in range(4)])
                for h in range(H):
                    if h % 8 == 0:
                        wait(pe, s_tp_free, c.tp.value(1 - h // 8))
                    pair, off = h // 2, h % 2 * DH

                    def emit(to):
                        for j in range(KD):
                            at = pair * D + j * P
                            done = nc.tensor.matmul(to[:, j * P:(j + 1) * P], wk1[off:off + DH, at:at + P],
                                                    qT1[off:off + DH, pair * P:(pair + 1) * P], start=True, stop=True)
                        return done
                    pe_project(pe, c, emit)

            def scores(b, rows):
                for rt in rows:
                    c.p.add()
                    wait(pe, s_p, c.p.value(4))
                    for j in range(KD):
                        done = nc.tensor.matmul(bank[SCORE + rt][:, 0:NCTX], qpv[:, j, b, rt * P:(rt + 1) * P],
                                                ctxT[b % 2][:, j * NCTX:(j + 1) * NCTX], start=(j == 0), stop=(j == KD - 1))
                    done.then_inc(s_s, 1)

            def wait_ctx(b):
                c.ctx[b % 2].add(48)
                wait(pe, s_ctx[b % 2], c.ctx[b % 2].value())

            def values(b):
                c.norm.add()
                wait(pe, s_norm, c.norm.value())
                for kc in range(2):
                    pe_transpose(pe, c, [p1[:, rt * NCTX + kc * P:rt * NCTX + (kc + 1) * P] for rt in range(4)])

                def mix(rt):
                    def emit(to):
                        for kc in range(2):
                            done = nc.tensor.matmul(to, pT1[:, (kc * 4 + rt) * P:(kc * 4 + rt + 1) * P],
                                                    ctxr[b % 2][:, kc * D:(kc + 1) * D], start=(kc == 0), stop=(kc == 1))
                        return done
                    pe_project(pe, c, emit)

                def turn(rt, behind):
                    wait(pe, s_proj_free, c.proj.value(behind))
                    pe_transpose(pe, c, [u[rt % 2][:, j * P:(j + 1) * P] for j in range(KD)])
                wait(pe, s_tp_free, c.tp.value())
                mix(0)
                mix(1)
                turn(0, 1)
                mix(2)
                turn(1, 1)
                mix(3)
                turn(2, 1)
                turn(3, 0)

            def out_heads():
                wait(pe, s_tp_free, c.tp.value())
                w = wv1.rearrange("p (k n) -> p k n", k=KD)
                for half_ in range(2):
                    def emit(to):
                        for h in range(half_ * 8, half_ * 8 + 8):
                            for j in range(KD):
                                done = nc.tensor.matmul(to[:, h % 8 * DH:(h % 8 + 1) * DH], utv[:, j, h, :],
                                                        w[:, j, h * DH:(h + 1) * DH], start=(j == 0), stop=(j == KD - 1))
                        return done
                    pe_project(pe, c, emit)

            def turn_out():
                wait(pe, s_proj_free, c.proj.value())
                for half_ in range(2):
                    pe_transpose(pe, c, [o1[:, (half_ * 4 + j) * P:(half_ * 4 + j + 1) * P] for j in range(4)])

            def project_out(turned):
                wait(pe, s_tp_free, turned)
                w = wo1.rearrange("p (k n) -> p k n", k=HD // P)

                def emit(to):
                    for j in range(HD // P):
                        done = nc.tensor.matmul(to, oT1[:, j * P:(j + 1) * P], w[:, j, :],
                                                start=(j == 0), stop=(j == HD // P - 1))
                    return done
                pe_project(pe, c, emit)

            def tile(final):
                for b in range(SEQS - 1):
                    wait_ctx(b + 1)
                    scores(b + 1, range(4))
                    values(b)
                if not final:
                    queries()
                values(SEQS - 1)
                out_heads()
                if not final:
                    wait_ctx(0)
                    scores(0, range(2))
                turn_out()
                turned = c.tp.value()
                if not final:
                    scores(0, range(2, 4))
                project_out(turned)

            for name in ("q1", "k1", "v1", "o1"):
                pe.wait_ge(s_w[name], 16)
            queries()
            wait(pe, s_proj_free, c.proj.value())
            wait_ctx(0)
            scores(0, range(4))
            with rounds(pe, TILES - 1, [(c.xn, 1), (c.proj, CROSS_TILE), (c.tp, 4 + 6 * SEQS), (c.p, 4 * SEQS),
                                        (c.norm, SEQS), (c.ctx[0], 96), (c.ctx[1], 96)]):
                tile(False)
            tile(True)

        def moe1_pe(pe, c):
            pe.wait_ge(s_w["experts1"], 16 * EXPERTS1)
            pe.wait_ge(s_w["tables1"], 16 * TABLES1)
            wait(pe, s_proj_free, c.proj.value())

            def tile():
                pe_turn_xn(pe, c, 2, 4)
                wait(pe, s_proj_free, c.proj.value())

                def product(w, n):
                    def emit(to):
                        for j in range(KD):
                            done = nc.tensor.matmul(to[:, 0:n], xnT[:, j * P:(j + 1) * P], w[:, j * n:(j + 1) * n],
                                                    start=(j == 0), stop=(j == KD - 1))
                        return done
                    pe_project(pe, c, emit, 4)
                product(router1, EXPERTS1)
                for e in range(EXPERTS1):
                    product(wexp1[:, e * W1:(e + 1) * W1], D)
                c.wmat.add()
                wait(pe, s_wmat, c.wmat.value())
                pe_transpose(pe, c, [wmat])
                wait(pe, s_tp_free, c.tp.value())
                pe_project(pe, c, lambda to: nc.tensor.matmul(to, wT[0:EXPERTS1, :], bexp[0:EXPERTS1, :],
                                                              start=True, stop=True), 4)
            with rounds(pe, TILES // 2, [(c.xn, 2), (c.proj, 24), (c.tp, 2), (c.wmat, 2)]):
                tile()
                tile()

        def layernorm(dve, i, free=None):
            xt = x[:, bass.ds(i * D, D)]
            dve.drain()
            if free:
                wait(dve, *free)
            nc.vector.bn_stats(stats, xt)
            dve.drain()
            nc.vector.bn_aggr(mv, stats)
            dve.drain()
            nc.vector.tensor_scalar(var, mv[:, 1:2], EPS, None, ALU.add)
            dve.drain()
            nc.vector.tensor_single_scalar(half.bitcast(I32), var.bitcast(I32), 1, ALU.logical_shift_right)
            dve.drain()
            nc.vector.tensor_scalar(root.bitcast(I32), half.bitcast(I32), -1.0, float(0x5F3759DF), ALU.mult, ALU.add)
            for _ in range(3):
                dve.drain()
                nc.vector.scalar_tensor_tensor(step, root, var, root, ALU.mult, ALU.mult)
                dve.drain()
                nc.vector.tensor_scalar(step, step, -0.5, 1.5, ALU.mult, ALU.add)
                dve.drain()
                nc.vector.tensor_tensor(root, root, step, ALU.mult)
            dve.drain()
            nc.vector.tensor_scalar(xn, xt, mv[:, 0:1], root, ALU.subtract, ALU.mult).then_inc(s_xn, 1)

        def dve_take(dve, c, op, banks=2):
            c.proj.add()
            wait(dve, s_proj, c.proj.value())
            op(bank[PROJ + (c.proj.n - 1) % banks]).then_inc(s_proj_free, 1)

        def dve_take_xn(dve, c, parts, banks=2):
            n = D // parts
            for part in range(parts):
                dve_take(dve, c, lambda src: nc.vector.tensor_copy(xnT[:, part * n:(part + 1) * n], src[:, 0:n]), banks)

        def heads(st, ap):
            return ap.rearrange("p (r c) -> p c r", r=st.rows).unsqueeze(3).broadcast_to(
                [P, H // st.rows, st.rows, st.dh])

        def by_head(st, ap):
            return ap.rearrange("p (c r n) -> p c r n", r=st.rows, n=st.dh)

        def attention_dve(dve, st, c):
            def take(blocks):
                for which, half_ in blocks:
                    part = slice(half_ * BANK, (half_ + 1) * BANK)

                    def op(src):
                        if which in "qk" and st.rope:
                            to, at = {"q": (q, 0), "k": (k, 2 * D)}[which]
                            cos, sin = rope[:, at:at + D], rope[:, at + D:at + 2 * D]
                            swapped = gate[:, 0:D] if which == "q" else gate[:, D:2 * D]
                            turned = swapped.rearrange("p (n two) -> p n two", two=2)
                            pairs, sins = (a.rearrange("p (n two) -> p n two", two=2) for a in (src, sin))
                            nc.vector.tensor_tensor(to[:, part], src, cos, ALU.mult)
                            for n in range(2):
                                nc.vector.tensor_tensor(turned[:, :, n], pairs[:, :, 1 - n], sins[:, :, n], ALU.mult)
                            dve.drain()
                            return nc.vector.tensor_tensor(to[:, part], to[:, part], swapped, ALU.add)
                        if which == "q":
                            if st.cross:
                                return nc.vector.scalar_tensor_tensor(q[:, part], src, st.dh ** -0.5, bq0[:, part],
                                                                      ALU.mult, ALU.add)
                            return nc.vector.tensor_scalar(q[:, part], src, st.dh ** -0.5, None, ALU.mult)
                        if which == "gate":
                            return nc.vector.tensor_scalar(gate[:, part], src, -1.0, None, ALU.mult)
                        if which == "rest":
                            return nc.vector.scalar_tensor_tensor(vrest[:, part], bv0[:, part], float(TAIL), src,
                                                                  ALU.mult, ALU.add)
                        to = {"k": k, "v": v}[which]
                        if st.cross:
                            return nc.vector.tensor_tensor(to[:, part], src, {"k": bk0, "v": bv0}[which][:, part], ALU.add)
                        return nc.vector.tensor_copy(to[:, part], src)
                    dve_take(dve, c, op)
                if blocks is st.late and st.gated:
                    dve.drain()
                    nc.vector.tensor_copy(step, step).then_inc(s_gate, 1)

            def sum_tails():
                for b in range(SEQS):
                    c.tail.add(16)
                    wait(dve, s_tail, c.tail.value())
                    nc.vector.tensor_reduce(csum[:, b:KD * SEQS:SEQS], tail.rearrange("p (k n) -> p k n", k=KD),
                                            AX.X, ALU.add).then_inc(s_tail_used, 1)
                dve.drain()
                nc.vector.tensor_copy(rest.rearrange("p (c n) -> p c n", n=S),
                                      csum.unsqueeze(2).broadcast_to([P, KD * SEQS, S])).then_inc(s_rest, 1)

            def mask_scores(i):
                if st.cross:
                    km = keymask[:, bass.ds(i * S, S)]
                    nc.vector.tensor_tensor(blockmask.rearrange("p (b n) -> p b n", b=SEQS),
                                            causal.rearrange("p (b n) -> p b n", b=SEQS),
                                            km.unsqueeze(1).broadcast_to([P, SEQS, S]), ALU.min)
                    dve.drain()
                for m, g in enumerate(st.order):
                    c.s.add()
                    wait(dve, s_s, c.s.value())
                    part = s[:, 4 * g * P:4 * (g + 1) * P].rearrange("p (h n) -> p h n", h=4)
                    if st.rope:
                        mask = alibi[:, 4 * g * P:4 * (g + 1) * P].rearrange("p (h n) -> p h n", h=4)
                    else:
                        mask = (blockmask if st.cross else apart).unsqueeze(1).broadcast_to([P, 4, P])
                    nc.vector.tensor_tensor(part, bank[SCORE + g].rearrange("p (h n) -> p h n", h=4), mask, ALU.add)
                    dve.drain()
                    done = nc.vector.tensor_reduce(negmax[:, 4 * g:4 * g + 4], part, AX.X, ALU.max, negate=True)
                    if m == 3 and st.cross:
                        dve.drain()
                        done = nc.vector.tensor_scalar(restp, negmax, MASKED, None, ALU.add)
                    done.then_inc(s_sm, 1)

            def take_out():
                c.p.add(4)
                wait(dve, s_p, c.p.value())
                if st.cross:
                    nc.vector.scalar_tensor_tensor(total, restp, float(TAIL), total, ALU.mult, ALU.add)
                    dve.drain()
                nc.vector.reciprocal(inv, total)
                dve.drain()
                of = heads(st, inv)
                ov = by_head(st, o[:, 0:st.width])
                src = by_head(st, psum[:, SCORE * BANK:SCORE * BANK + st.width])
                if st.cross:
                    nc.vector.tensor_tensor(restp, restp, inv, ALU.mult)
                    dve.drain()
                    vr = by_head(st, vrest)
                    nc.vector.tensor_tensor(vr, vr, heads(st, restp), ALU.mult)
                if st.gated:
                    c.gate.add()
                    wait(dve, s_gate_exp, c.gate.value())
                    nc.vector.tensor_scalar(gate, gate, 1.0, None, ALU.add)
                    dve.drain()
                    nc.vector.reciprocal(gate, gate)
                    dve.drain()
                    gv = by_head(st, gate)
                    nc.vector.tensor_tensor(gv, gv, of, ALU.mult)
                    dve.drain()
                    of = gv
                c.o.add()
                wait(dve, s_o, c.o.value())
                done = nc.vector.tensor_tensor(ov, src, of, ALU.mult)
                if st.cross:
                    dve.drain()
                    done = nc.vector.tensor_tensor(o, o, vrest, ALU.add)
                done.then_inc(s_o_ready, 1)

            def add_to_x(i):
                xt = x[:, bass.ds(i * D, D)]
                dve_take(dve, c, lambda src: nc.vector.tensor_tensor(xt, xt, src, ALU.add))
                if st.cross:
                    dve.drain()
                    nc.vector.tensor_tensor(xt, xt, bo0, ALU.add)

            if st.rope:
                dve.wait_ge(s_w["rope"], 16)
                dve.wait_ge(s_w["alibi"], 16)
            if st.cross:
                sum_tails()
            dve_take_xn(dve, c, st.parts)
            take(st.early)
            take(st.late)
            layernorm(dve, 1)
            mask_scores(0)
            counts = [(c.proj, st.per_proj), (c.s, 4), (c.p, 4), (c.o, 1)]
            if st.cross:
                counts += [(c.tail, 16 * SEQS)]
            if st.gated:
                counts += [(c.gate, 1)]
            with rounds(dve, TILES - 1, counts) as i:
                if st.cross:
                    sum_tails()
                dve_take_xn(dve, c, st.parts)
                take(st.early)
                take_out()
                take(st.late)
                layernorm(dve, (i + 2) % TILES)
                mask_scores(i + 1)
                add_to_x(i)
            take_out()
            add_to_x(TILES - 1)
            dve.drain()
            nc.vector.tensor_copy(step, step).then_inc(s_end[st.name], 1)

        def route_dve(dve, c):
            def choose(i):
                dve_take_xn(dve, c, 2)
                dve_take(dve, c, lambda src: nc.vector.tensor_copy(logit, src[:, 0:EXPERTS]))
                dve.drain()
                nc.vector.tensor_reduce(top, logit, AX.X, ALU.max, negate=True).then_inc(s_logit, 1)
                c.route.add()
                wait(dve, s_exp, c.route.value())
                nc.vector.reciprocal(rinv, rsum)
                dve.drain()
                nc.vector.tensor_scalar(prob, prob, rinv, None, ALU.mult)
                dve.drain()
                nc.vector.max(ranked, prob)
                dve.drain()
                nc.vector.max_index(chosen_u, ranked, prob)
                nc.vector.tensor_reduce(rsum, ranked, AX.X, ALU.add)
                dve.drain()
                nc.vector.tensor_copy(wrest[:, 0:TOPK], chosen_u)
                nc.vector.reciprocal(rinv, rsum)
                dve.drain()
                eqv = eq.rearrange("p (r e) -> p r e", r=TOPK)
                nc.vector.tensor_tensor(eqv, iota64.unsqueeze(1).broadcast_to([P, TOPK, EXPERTS]),
                                        wrest[:, 0:TOPK].unsqueeze(2).broadcast_to([P, TOPK, EXPERTS]), ALU.is_equal)
                dve.drain()
                nc.vector.tensor_reduce(sel, eq.rearrange("p (r e) -> p e r", r=TOPK), AX.X, ALU.add)
                dve.drain()
                nc.vector.tensor_copy(selb, sel).then_inc(s_sel, 1)
                nc.vector.scalar_tensor_tensor(wsel, prob, rinv, sel, ALU.mult, ALU.mult)
                info = slotinfo[:, bass.ds(i * EXPERTS * INFO, EXPERTS * INFO)].rearrange("p (e n) -> p e n", n=INFO)
                for n in range(3):
                    dve.drain()
                    nc.vector.tensor_copy(info[:, :, 3 + n], wsel)
                    if n < 2:
                        dve.drain()
                        nc.vector.tensor_tensor(wsel, wsel, info[:, :, 3 + n], ALU.subtract)
                nc.vector.tensor_scalar(sel, sel, -float(UNSEEN), float(UNSEEN), ALU.mult, ALU.add)
                dve.drain()
                dve_take(dve, c, lambda src: nc.vector.tensor_tensor(posm[:, bass.ds(i * EXPERTS, EXPERTS)], src[:, 0:EXPERTS],
                                                                     sel, ALU.add))
                nc.vector.tensor_tensor(cumb, cumb, selb, ALU.add)

            dve.wait_ge(s_w["tables0"], 16 * TABLES0)
            nc.vector.memset(cumb, 0.0)
            infov = slotinfo.rearrange("p (t e n) -> p t e n", t=TILES, e=EXPERTS)
            for j in range(TILES):
                nc.vector.tensor_copy(infov[:, j, :, 0:3], tokens[:, 3 * j:3 * j + 3].unsqueeze(1).broadcast_to([P, EXPERTS, 3]))
            dve.drain()
            with rounds(dve, TILES - 1, [(c.proj, ROUTE_PROJ), (c.route, 1)]) as i:
                choose(i)
                layernorm(dve, i + 1, (s_xn_d, i * 16 + 16))
            choose(TILES - 1)
            dve.drain()

        def experts_dve(dve, c):
            posv = posm.rearrange("p (t e) -> p t e", t=TILES)

            def ask(e, r):
                wait(dve, s_idx, 4 * r + e - 1)
                at = 4 * r + e
                if isinstance(at, int):
                    place = posv[:, :, at:at + 1]
                else:
                    place = posm[:, bass.ds(at, (TILES - 1) * EXPERTS + 1)][:, 0::EXPERTS].unsqueeze(2)
                nc.vector.tensor_tensor(onehot[e % 2].rearrange("p (t n) -> p t n", t=TILES),
                                        iota128.unsqueeze(1).broadcast_to([P, TILES, CAP]),
                                        place.broadcast_to([P, TILES, CAP]), ALU.is_equal).then_inc(s_onehot, 1)

            def answer(e, r):
                n = e % SLOTS
                wait(dve, s_scatter, 64 * r + 16 * (e - SLOTS) + 16)
                wait(dve, s_idx, 4 * r + e + 1)
                src = bank[7]
                nc.vector.tensor_copy(fidx, src[:, 0:1])
                nc.vector.tensor_scalar(empty, src[:, 2:3], -float(NOWHERE), float(NOWHERE), ALU.mult, ALU.add)
                nc.vector.tensor_copy(wslot[:, n:n + 1], src[:, 3:4])
                dve.drain()
                nc.vector.scalar_tensor_tensor(fidx, src[:, 1:2], float(P), fidx, ALU.mult, ALU.add)
                nc.vector.tensor_tensor(wslot[:, n:n + 1], src[:, 4:5], wslot[:, n:n + 1], ALU.add)
                dve.drain()
                nc.vector.tensor_copy(gidx.bitcast(U32)[:, n:n + 1], fidx)
                nc.vector.tensor_tensor(sidx.bitcast(U32)[:, n:n + 1], fidx, empty, ALU.add)
                nc.vector.tensor_tensor(wslot[:, n:n + 1], src[:, 5:6], wslot[:, n:n + 1], ALU.add).then_inc(s_slot, 1)

            def silu_up(e, r):
                wait(dve, s_gexp, 4 * r + e + 1)
                nc.vector.tensor_scalar(gexp, gexp, 1.0, None, ALU.add)
                dve.drain()
                nc.vector.reciprocal(gexp, gexp)
                dve.drain()
                nc.vector.tensor_tensor(gexp, gexp, bank[e % 2 * 2][:, 0:INTER], ALU.mult)
                dve.drain()
                wait(dve, s_gu, 4 * r + e + 1)
                nc.vector.tensor_tensor(hid, gexp, bank[e % 2 * 2 + 1][:, 0:INTER], ALU.mult).then_inc(s_h, 1)

            def take_down(e, r):
                wait(dve, s_scatter, 64 * r + 16 * (e - 2) + 16)
                wait(dve, s_y, 4 * r + e + 1)
                nc.vector.tensor_scalar(y[e % 2], bank[6], wslot[:, e % SLOTS:e % SLOTS + 1], None,
                                        ALU.mult).then_inc(s_y_ready, 1)

            for e in range(3):
                ask(e, 0)
                answer(e, 0)

            def four(r, first, final):
                for e in range(SLOTS):
                    silu_up(e, r)
                    if not (final and e >= 1):
                        ask(e + 3, r)
                        answer(e + 3, r)
                    take_down(e, r)
            four(0, True, False)
            with dve.Fori(1, EXPERTS // SLOTS - 1) as r:
                four(r, False, False)
            four(EXPERTS // SLOTS - 1, False, True)

        def cross_dve(dve, c):
            def queries():
                dve_take_xn(dve, c, 1)
                for half_ in range(2):
                    part = slice(half_ * BANK, (half_ + 1) * BANK)
                    dve_take(dve, c, lambda src: nc.vector.scalar_tensor_tensor(
                        q1[:, part], src, DH ** -0.5, bq1[:, part], ALU.mult, ALU.add))
                qpv = qp.rearrange("p (c b h n) -> p c b h n", c=KD, b=SEQS, h=H)
                for h in range(H):
                    dve_take(dve, c, lambda src: nc.vector.tensor_copy(
                        qpv[:, :, :, h, :], src.rearrange("p (c b n) -> p c b n", c=KD, b=SEQS)))
                nc.vector.tensor_tensor(uu, q1, bk1, ALU.mult)
                dve.drain()
                nc.vector.tensor_reduce(ctok, uu.rearrange("p (h n) -> p h n", h=H), AX.X, ALU.add)
                dve.drain()
                for b in range(SEQS):
                    for n in range(4):
                        nc.vector.tensor_copy(crow[n * S:(n + 1) * S, b * 4:b * 4 + 4], ctok[b * S:(b + 1) * S, n::4])

            def maxima(b):
                for rt in range(4):
                    c.s.add()
                    wait(dve, s_s, c.s.value())
                    nc.vector.tensor_reduce(negmax[:, rt:rt + 1], bank[SCORE + rt][:, 0:NCTX], AX.X, ALU.max, negate=True)
                dve.drain()
                cb = crow[:, b * 4:b * 4 + 4]
                nc.vector.tensor_tensor(negc, negmax[:, 0:4], cb, ALU.subtract)
                dve.drain()
                nc.vector.tensor_tensor(negc, negc, cb, ALU.add).then_inc(s_sm, 1)

            def normalise():
                c.p.add(4)
                wait(dve, s_p, c.p.value())
                nc.vector.reciprocal(inv[:, 0:4], total1)
                dve.drain()
                pv = p1.rearrange("p (r n) -> p r n", r=4)
                nc.vector.tensor_tensor(plast, pv[:, :, NCTX - 1], inv[:, 0:4], ALU.mult)
                pv = pv[:, :, 0:NCTX - 1]
                nc.vector.tensor_tensor(pv, pv, inv[:, 0:4].unsqueeze(2).broadcast_to([P, 4, NCTX - 1]), ALU.mult).then_inc(s_norm, 1)

            def take_rows(b):
                for rt in range(4):
                    dve_take(dve, c, lambda src: nc.vector.scalar_tensor_tensor(
                        u[rt % 2], ctxl[b % 2], plast[:, rt:rt + 1], src, ALU.mult, ALU.add))

            def take_heads():
                for half_ in range(2):
                    part = slice(half_ * BANK, (half_ + 1) * BANK)
                    dve_take(dve, c, lambda src: nc.vector.tensor_tensor(o1[:, part], src, bv1[:, part], ALU.add))

            def add_to_x(i):
                xt = x[:, bass.ds(i * D, D)]
                dve_take(dve, c, lambda src: nc.vector.tensor_tensor(xt, xt, src, ALU.add))
                dve.drain()
                nc.vector.tensor_tensor(xt, xt, bo1, ALU.add)

            def tile(i, final):
                for b in range(SEQS - 1):
                    maxima(b + 1)
                    take_rows(b)
                    normalise()
                if not final:
                    queries()
                take_rows(SEQS - 1)
                take_heads()
                layernorm(dve, (i + 2) % TILES) if not final else None
                if not final:
                    maxima(0)
                    normalise()
                add_to_x(i)

            dve.wait_ge(s_x_back[0], 16)
            layernorm(dve, 0)
            dve.wait_ge(s_w["bias1"], 16 * 3)
            nc.vector.tensor_scalar(bq1, bq1, DH ** -0.5, None, ALU.mult)
            dve.drain()
            queries()
            dve.wait_ge(s_x_back[1], 16)
            layernorm(dve, 1)
            dve.wait_ge(s_w["bo1"], 16)
            maxima(0)
            normalise()
            with rounds(dve, TILES - 1, [(c.proj, CROSS_TILE), (c.s, 4 * SEQS), (c.p, 4 * SEQS)]) as i:
                tile(i, False)
            tile(TILES - 1, True)
            dve.drain()
            nc.vector.tensor_copy(step, step).then_inc(s_end["xattn1"], 1)

        def moe1_dve(dve, c):
            dve.wait_ge(s_w["tables1"], 16 * TABLES1)
            nc.vector.memset(wmat, 0.0)
            dve.drain()

            def tile(i):
                xt = x[:, bass.ds(i * D, D)]
                dve_take_xn(dve, c, 2, 4)
                dve_take(dve, c, lambda src: nc.vector.tensor_tensor(logit1, src[:, 0:EXPERTS1], brouter, ALU.add), 4)
                dve.drain()
                nc.vector.tensor_reduce(top, logit1, AX.X, ALU.max, negate=True).then_inc(s_logit, 1)
                c.route.add()
                wait(dve, s_exp, c.route.value())
                nc.vector.reciprocal(rinv, rsum)
                dve.drain()
                nc.vector.tensor_scalar(prob1, prob1, rinv, None, ALU.mult)
                dve.drain()
                nc.vector.max(ranked1, prob1)
                dve.drain()
                nc.vector.max_index(chosen1.bitcast(U32), ranked1, prob1)
                dve.drain()
                nc.vector.tensor_copy(logit1, chosen1.bitcast(U32))
                dve.drain()
                wm = wmat[:, 0:EXPERTS1]
                nc.vector.tensor_scalar(wm, iota8, logit1[:, 0:1], ranked1[:, 0:1], ALU.is_equal, ALU.mult)
                nc.vector.tensor_scalar(pick, iota8, logit1[:, 1:2], ranked1[:, 1:2], ALU.is_equal, ALU.mult)
                dve.drain()
                nc.vector.tensor_tensor(wm, wm, pick, ALU.add).then_inc(s_wmat, 1)
                layernorm(dve, (i + 1) % TILES)
                for e in range(EXPERTS1):
                    dve.drain()
                    dve_take(dve, c, lambda src: nc.vector.scalar_tensor_tensor(xt, src, wmat[:, e:e + 1], xt, ALU.mult, ALU.add), 4)
                dve.drain()
                dve_take(dve, c, lambda src: nc.vector.tensor_tensor(xt, xt, src, ALU.add), 4)
                dve.drain()
                nc.vector.tensor_copy(step, step).then_inc(s_final, 1)
            with rounds(dve, TILES // 2, [(c.proj, 24), (c.route, 2)]) as i:
                tile(i * 2)
                tile(i * 2 + 1)

        def act_take(act, c, to):
            c.tp.add()
            wait(act, s_tp, c.tp.value())
            src = bank[TP + (c.tp.n - 1) % 2]
            nc.scalar.copy(to, src[:, 0:to.free_size()]).then_inc(s_tp_free, 1)

        def attention_act(act, st, c):
            def take_qk():
                for to in (qT, kT):
                    for half_ in range(st.halves):
                        act_take(act, c, to[:, half_ * BANK:(half_ + 1) * BANK])

            def exps():
                if st.gated:
                    c.gate.add()
                    wait(act, s_gate, c.gate.value())
                    nc.scalar.activation(gate, gate, ACT.Exp).then_inc(s_gate_exp, 1)
                for m, g in enumerate(st.order):
                    c.sm.add()
                    wait(act, s_sm, c.sm.value())
                    if m == 3 and st.cross:
                        nc.scalar.activation(restp, restp, ACT.Exp)
                    for n in range(4 * g, 4 * g + 4):
                        part = s[:, n * P:(n + 1) * P]
                        done = nc.scalar.activation(part, part, ACT.Exp, bias=negmax[:, n:n + 1],
                                                    accum_out=total[:, n:n + 1])
                    done.then_inc(s_p, 1)

            def take_probs():
                for g in st.order:
                    act_take(act, c, pT[:, 4 * g * P:4 * (g + 1) * P])

            def take_out():
                n = st.width // 2
                for part in range(2):
                    act_take(act, c, oT[:, part * n:(part + 1) * n])

            take_qk()
            exps()
            counts = [(c.tp, st.per_tp), (c.sm, 4)]
            if st.gated:
                counts += [(c.gate, 1)]
            with rounds(act, TILES - 1, counts):
                take_probs()
                take_qk()
                take_out()
                exps()
            take_probs()
            take_out()

        def route_act(act, c):
            with rounds(act, TILES, [(c.route, 1)]) as i:
                act.wait_ge(s_xn, i + 2 * TILES + 1)
                act.dma_start(xn_d[bass.ds(i * P, P), :], xn).then_inc(s_xn_d, 16)
                c.route.add()
                wait(act, s_logit, c.route.value())
                nc.scalar.activation(prob, logit, ACT.Exp, bias=top, accum_out=rsum).then_inc(s_exp, 1)

        def experts_act(act, c):
            def turned(e, r):
                wait(act, s_xgt, 4 * r + e + 1)
                nc.scalar.copy(xgT[e % 2], bank[4]).then_inc(s_xgt_free, 1)

            def exp(e, r):
                wait(act, s_h, 4 * r + e)
                wait(act, s_g, 4 * r + e + 1)
                nc.scalar.activation(gexp, bank[e % 2 * 2][:, 0:INTER], ACT.Exp, scale=-1.0).then_inc(s_gexp, 1)

            def hidden(e, r):
                wait(act, s_ht, 4 * r + e + 1)
                nc.scalar.copy(hidT, bank[5][:, 0:INTER]).then_inc(s_ht_free, 1)

            def four(r, final):
                for e in range(SLOTS):
                    if not (final and e == 3):
                        turned(e + 1, r)
                        exp(e + 1, r)
                    hidden(e, r)
            turned(0, 0)
            exp(0, 0)
            with act.Fori(0, EXPERTS // SLOTS - 1) as r:
                four(r, False)
            four(EXPERTS // SLOTS - 1, True)

        def cross_act(act, c):
            utv = ut.rearrange("p (c h n) -> p c h n", c=KD, h=H)

            def take_q():
                for half_ in range(2):
                    act_take(act, c, qT1[:, half_ * BANK:(half_ + 1) * BANK])

            def exps():
                c.sm.add()
                wait(act, s_sm, c.sm.value())
                for rt in range(4):
                    nc.scalar.activation(p1[:, rt * NCTX:(rt + 1) * NCTX], bank[SCORE + rt][:, 0:NCTX], ACT.Exp,
                                         bias=negc[:, rt:rt + 1], accum_out=total1[:, rt:rt + 1]).then_inc(s_p, 1)

            def take_weights():
                for kc in range(2):
                    act_take(act, c, pT1[:, kc * 4 * P:(kc + 1) * 4 * P])

            def take_rows(b):
                for rt in range(4):
                    c.tp.add()
                    wait(act, s_tp, c.tp.value())
                    src = bank[TP + (c.tp.n - 1) % 2].rearrange("p (c h n) -> p c h n", c=KD, h=4)
                    nc.scalar.copy(utv[:, :, 4 * rt:4 * rt + 4, b * S:(b + 1) * S], src).then_inc(s_tp_free, 1)

            def take_out():
                for half_ in range(2):
                    act_take(act, c, oT1[:, half_ * BANK:(half_ + 1) * BANK])

            def tile(final):
                for b in range(SEQS - 1):
                    take_weights()
                    exps()
                    take_rows(b)
                if not final:
                    take_q()
                take_weights()
                take_rows(SEQS - 1)
                take_out()
                if not final:
                    exps()
            take_q()
            exps()
            with rounds(act, TILES - 1, [(c.tp, 4 + 6 * SEQS), (c.sm, SEQS)]):
                tile(False)
            tile(True)

        def moe1_act(act, c):
            def tile():
                c.route.add()
                wait(act, s_logit, c.route.value())
                nc.scalar.activation(prob1, logit1, ACT.Exp, bias=top, accum_out=rsum).then_inc(s_exp, 1)
                act_take(act, c, wT)
            with rounds(act, TILES // 2, [(c.tp, 2), (c.route, 2)]):
                tile()
                tile()

        TABLES0, TABLES1 = 6, 4
        @block.tensor
        def _(pe):
            c = Counts()
            pe.wait_ge(s_const, 16 * 4)
            attention_pe(pe, xattn0, c)
            attention_pe(pe, attn0, c)
            route_pe(pe, c)
            experts_pe(pe, c)
            cross_pe(pe, c)
            attention_pe(pe, attn1, c)
            moe1_pe(pe, c)

        @block.vector
        def _(dve):
            c = Counts()
            dve.wait_ge(s_const, 16 * 4)
            dve.wait_ge(s_w["bias0"], 16 * 4)
            nc.vector.tensor_scalar(bq0, bq0, DH ** -0.5, None, ALU.mult)
            nc.vector.tensor_scalar(keymask, keymask_u8.bitcast(U8), MASKED, None, ALU.mult)
            dve.wait_ge(s_x, 16)
            layernorm(dve, 0)
            attention_dve(dve, xattn0, c)
            attention_dve(dve, attn0, c)
            route_dve(dve, c)
            experts_dve(dve, c)
            cross_dve(dve, c)
            attention_dve(dve, attn1, c)
            moe1_dve(dve, c)

        @block.scalar
        def _(act):
            c = Counts()
            attention_act(act, xattn0, c)
            attention_act(act, attn0, c)
            route_act(act, c)
            experts_act(act, c)
            cross_act(act, c)
            attention_act(act, attn1, c)
            moe1_act(act, c)

        @block.gpsimd
        def _(pool):
            def load_head(i):
                pool.dma_start(ctxh, t["ctx_head"][bass.ds(i * P, P), :]).then_inc(s_ctxh, 16)

            def load_tail(b):
                pool.dma_start(tail, t["ctx_tail"][bass.ds(b * P, P), :]).then_inc(s_tail, 16)

            V_READ = xattn0.parts + len(xattn0.early) + xattn0.halves
            load_head(0)
            load_tail(0)
            for b in range(1, SEQS):
                pool.wait_ge(s_tail_used, b)
                load_tail(b)
            pool.wait_ge(s_proj, V_READ)
            load_head(1)
            with pool.Fori(0, TILES - 2) as i:
                for b in range(SEQS):
                    pool.wait_ge(s_tail_used, i * SEQS + SEQS + b)
                    load_tail(i * SEQS + SEQS + b)
                pool.wait_ge(s_proj, i * xattn0.per_proj + xattn0.per_proj - 1 + V_READ)
                load_head(i + 2)
            for b in range(SEQS):
                pool.wait_ge(s_tail_used, (TILES - 1) * SEQS + b)
                load_tail((TILES - 1) * SEQS + b)

            def load(to, name, k, s_):
                pool.dma_start(to.rearrange("p (k n) -> p k n", k=k),
                               t[name].rearrange("(k p) n -> p k n", p=P)).then_inc(s_, 16)

            pool.wait_ge(s_end["attn0"], 1)
            load(router0, "router0", KD, s_w["tables0"])
            for to, name in ((iota64, "iota64"), (iota128, "iota128"), (tokens, "tokens")):
                pool.dma_start(to, t[name]).then_inc(s_w["tables0"], 16)
            for to, name in ((tri, "tri"), (ones, "ones")):
                pool.dma_start(to, t[name]).then_inc(s_w["tables0"], 16)
            pool.dma_start(x_d.rearrange("(t p) d -> p t d", p=P), x.rearrange("p (t d) -> p t d", t=TILES)).then_inc(s_x_d, 16)
            load(wq1, "q1", KD, s_w["q1"])
            load(wk1, "k1", HD // P, s_w["k1"])
            load(wv1, "v1", KD, s_w["v1"])
            pool.dma_start(bo1, t["bo1"].partition_broadcast(P)).then_inc(s_w["bo1"], 16)
            pool.wait_ge(s_xn_d, 16 * TILES)
            pool.wait_ge(s_x_d, 16)
            nc.gpsimd.memset(zero, 0.0)
            pool.drain()

            holds = Count()

            def hold():
                wait(pool, s_held, holds.value())
                nc.gpsimd.tensor_tensor(held, zero, zero, ALU.add).then_inc(s_held, 1)
                holds.add()

            def gather(e, r):
                pool.wait_ge(s_slot, 4 * r + e + 1)
                wait(pool, s_xgt, 4 * r + e - 1)
                hold()
                pool.indirect_dma_start(xg[e % 2], None, xn_d, bass.IndirectOffsetOnAxis(
                    ap=gidx.bitcast(U32)[:, e % SLOTS:e % SLOTS + 1], axis=0)).then_inc(s_gather[e % 2], 16)

            def scatter(e, r):
                pool.wait_ge(s_y_ready, 4 * r + e + 1)
                wait(pool, s_scatter, 64 * r + 16 * e)
                hold()
                pool.indirect_dma_start(x_d, bass.IndirectOffsetOnAxis(
                    ap=sidx.bitcast(U32)[:, e % SLOTS:e % SLOTS + 1], axis=0), y[e % 2], None,
                    bounds_check=B * S - 1, oob_is_err=False, compute_op=ALU.add).then_inc(s_scatter, 16)

            def four(r, final):
                for e in range(SLOTS):
                    if not (final and e >= 2):
                        gather(e + 2, r)
                    scatter(e, r)
            gather(0, 0)
            gather(1, 0)
            four(0, False)
            with rounds(pool, EXPERTS // SLOTS - 2, [(holds, 2 * SLOTS)]) as r:
                four(r + 1, False)
            four(EXPERTS // SLOTS - 1, True)
            pool.wait_ge(s_scatter, 16 * EXPERTS)
            pool.dma_start(x[:, 0:D], x_d[0:P, :]).then_inc(s_x_back[0], 16)
            pool.dma_start(x[:, D:].rearrange("p (t d) -> p t d", t=TILES - 1),
                           x_d[P:, :].rearrange("(t p) d -> p t d", p=P)).then_inc(s_x_back[1], 16)
        @block.sync
        def _(sp):
            def load(to, name, k, s_):
                sp.dma_start(to.rearrange("p (k n) -> p k n", k=k),
                             t[name].rearrange("(k p) n -> p k n", p=P)).then_inc(s_, 16)

            def load_row(to, name, s_):
                sp.dma_start(to, t[name].partition_broadcast(P)).then_inc(s_, 16)

            load(x, "x", TILES, s_x)
            for to, name in ((ident, "ident"), (causal, "mask_causal"), (apart, "mask_apart")):
                sp.dma_start(to, t[name]).then_inc(s_const, 16)
            sp.dma_start(keymask_u8.bitcast(U8), t["mask"]).then_inc(s_const, 16)
            load(wq0, "q0", KD, s_w["q0"])
            load(wk0, "k0", KD, s_w["k0"])
            for to, name in ((bq0, "bq0"), (bk0, "bk0"), (bv0, "bv0"), (bo0, "bo0")):
                load_row(to, name, s_w["bias0"])
            load(wv0, "v0", KD, s_w["v0"])
            load(wo0, "o0", H * DH // P, s_w["o0"])
            load(wqkv0, "qkv0", 3 * KD, s_w["qkv0"])
            sp.wait_ge(s_proj, TILES * xattn0.per_proj - len(xattn0.late) - 1)
            load(wgate0, "gate0", KD, s_w["gate0"])
            load(wout0, "out0", HD // P, s_w["out0"])
            sp.wait_ge(s_end["xattn0"], 1)
            for j in range(SLOTS):
                if j == 2:
                    sp.wait_ge(s_end["attn0"], 1)
                sp.dma_start(slots[j], t["experts0"][j * P:(j + 1) * P, :]).then_inc(s_ew[j], 16)
            with sp.Fori(1, EXPERTS // SLOTS) as r:
                for j in range(SLOTS):
                    sp.wait_ge(s_y, r * 4 - 3 + j)
                    sp.dma_start(slots[j], t["experts0"][bass.ds((r * SLOTS + j) * P, P), :]).then_inc(s_ew[j], 16)
            sp.wait_ge(s_scatter, 16 * EXPERTS)
            for to, name in ((bq1, "bq1"), (bk1, "bk1"), (bv1, "bv1")):
                load_row(to, name, s_w["bias1"])

            def load_ctx(b, seq):
                n = b % 2
                sp.dma_start(ctxT[n], t["ctxT"][bass.ds(seq * P, P), :]).then_inc(s_ctx[n], 16)
                rows = t["ctx"][bass.ds(seq, 1), :, :]
                sp.dma_start(ctxr[n].rearrange("p (c d) -> p c d", c=2),
                             rows[:, 0:2 * P, :].rearrange("o (c p) d -> (o p) c d", p=P)).then_inc(s_ctx[n], 16)
                sp.dma_start(ctxl[n], rows[:, NCTX - 1, :].broadcast_to([P, D])).then_inc(s_ctx[n], 16)
            before = TILES * (xattn0.per_proj + attn0.per_proj + ROUTE_PROJ) + CROSS_PROJ
            used = [4, 8, 12, 16 + CROSS_PROJ]
            load_ctx(0, 0)
            load_ctx(1, 1)
            load(wo1, "o1", HD // P, s_w["o1"])
            for b in (2, 3):
                sp.wait_ge(s_proj_free, before + used[b - 2])
                load_ctx(b, b)
            with sp.Fori(1, TILES) as i:
                for b in range(SEQS):
                    sp.wait_ge(s_proj_free, (i - 1) * CROSS_TILE + before + used[b + 2] if b < 2
                               else i * CROSS_TILE + before + used[b - 2])
                    load_ctx(b, i * SEQS + b)
            sp.wait_ge(s_proj, before + (TILES - 2) * CROSS_TILE + used[2] + CROSS_PROJ)
            load(awq1, "aq1", KD, s_w["aq1"])
            load(awk1, "ak1", KD, s_w["ak1"])
            sp.dma_start(rope, t["rope"]).then_inc(s_w["rope"], 16)
            sp.dma_start(alibi, t["alibi"]).then_inc(s_w["alibi"], 16)
            sp.wait_ge(s_end["xattn1"], 1)
            load(awv1, "av1", KD, s_w["av1"])
            load(awo1, "ao1", KD, s_w["ao1"])
            for e in range(EXPERTS1):
                sp.dma_start(wexp1[:, e * W1:(e + 1) * W1], t["experts1"][e * P:(e + 1) * P, :]).then_inc(s_w["experts1"], 16)
            sp.wait_ge(s_end["attn1"], 1)
            load(router1, "router1", KD, s_w["tables1"])
            load_row(brouter, "brouter1", s_w["tables1"])
            load_row(iota8, "iota8", s_w["tables1"])
            sp.dma_start(bexp[0:EXPERTS1, :], t["bexp1"]).then_inc(s_w["tables1"], 16)
            with sp.Fori(0, TILES) as i:
                sp.wait_ge(s_final, i + 1)
                sp.dma_start(t["out"][bass.ds(i * P, P), :], x[:, bass.ds(i * D, D)]).then_inc(s_out, 16)
            sp.wait_ge(s_out, 16 * TILES)


def kernel(**inputs):
    import numpy as np
    from ml_dtypes import bfloat16 as bf16
    import concourse.bacc as bacc
    from concourse.bass_utils import run_bass_kernel_spmd

    a = {n: np.asarray(w) for n, w in inputs.items()}

    def transposed(w):
        return np.ascontiguousarray(np.swapaxes(w, -1, -2))

    ctx = a["ctx_1024"]
    ctxT = ctx.reshape(B, NCTX, KD, P).transpose(0, 3, 2, 1)
    token = np.arange(P)
    same = token[:, None] // S == token[None, :] // S
    seen = same & (token[:, None] >= token[None, :])
    mask_causal = np.where(seen, 0.0, np.where(same, MASKED, APART)).astype(np.float32)
    mask_apart = np.where(seen, 0.0, APART).astype(np.float32)
    qkv = a["L0_attn_w_qkv"].reshape(3, HD, D).transpose(0, 2, 1).reshape(3 * D, HD)
    arrays = {
        "x": a["x"].reshape(B * S, D),
        "ctx_head": ctxT[:, :, :, :S].reshape(TILES, SEQS, P, KD, S).transpose(0, 2, 3, 1, 4).reshape(TILES * P, D),
        "ctx_tail": ctxT[:, :, :, S:].reshape(B * P, KD * TAIL),
        "mask": np.repeat(a["mask_BxS2_bf0"][:, :S].reshape(TILES, SEQS, S).transpose(1, 0, 2),
                          S, axis=0).reshape(P, TILES * S),
        "q0": a["L0_xattn_Wq"], "k0": a["L0_xattn_Wk"], "v0": a["L0_xattn_Wv"], "o0": a["L0_xattn_Wo"],
        "bq0": a["L0_xattn_bq"], "bk0": a["L0_xattn_bk"], "bv0": a["L0_xattn_bv"], "bo0": a["L0_xattn_bo"],
        "qkv0": qkv, "gate0": transposed(a["L0_attn_w_gate"]), "out0": transposed(a["L0_attn_w_out"]),
        "ident": np.eye(P, dtype=np.float32), "mask_causal": mask_causal, "mask_apart": mask_apart,
    }
    def by_partition(w):
        n, rows, cols = w.shape
        return w.reshape(n, rows // P, P, cols).transpose(0, 2, 1, 3).reshape(n * P, rows // P * cols)

    dk = D // H
    inv_freq = (1.0 / 10000.0 ** (np.arange(0, dk, 2, dtype=np.float32) / dk)).astype(np.float32)
    freqs = (token % S).astype(np.float32)[:, None] * inv_freq[None, :]
    cos, sin = (np.tile(np.repeat(f(freqs), 2, axis=-1), (1, H)).astype(np.float32) for f in (np.cos, np.sin))
    sin = sin * np.tile(np.array([-1, 1], np.float32), D // 2)
    scale = np.float32(dk ** -0.5)
    places = Attention("attn1", dk, ()).places
    slopes = 2.0 ** (-8.0 * np.array(places, dtype=np.float32) / H)
    rel = -np.abs(token[:, None] - token[None, :]).astype(np.float32)
    alibi = np.where(same[:, None, :], slopes[None, :, None].astype(np.float32) * rel[:, None, :], APART)
    arrays.update({
        "experts0": np.concatenate([by_partition(transposed(a["L0_ffn_" + n])) for n in ("w_gate", "w_up", "w_down")], axis=1),
        "router0": transposed(a["L0_ffn_gate_w"]),
        "iota64": np.tile(np.arange(EXPERTS, dtype=np.float32), (P, 1)),
        "iota128": np.tile(np.arange(CAP, dtype=np.float32), (P, 1)),
        "tokens": np.stack([np.stack([token, np.full(P, j), np.ones(P)], -1) for j in range(TILES)], 1)
        .reshape(P, TILES * 3).astype(np.float32),
        "tri": (token[:, None] < token[None, :]).astype(bf16), "ones": np.ones((P, P), bf16),
        "q1": transposed(a["L1_xattn_Wq"]), "k1": a["L1_xattn_Wk"], "v1": transposed(a["L1_xattn_Wv"]),
        "o1": transposed(a["L1_xattn_Wo"]),
        "bq1": a["L1_xattn_bq"], "bk1": a["L1_xattn_bk"], "bv1": a["L1_xattn_bv"], "bo1": a["L1_xattn_bo"],
        "ctx": ctx, "ctxT": ctxT.reshape(B * P, KD * NCTX),
        "aq1": transposed(a["L1_attn_Wq"]), "ak1": transposed(a["L1_attn_Wk"]), "av1": transposed(a["L1_attn_Wv"]),
        "ao1": transposed(a["L1_attn_Wo"]),
        "rope": np.concatenate([cos * scale, sin * scale, cos, sin], axis=1).astype(np.float32),
        "alibi": alibi.reshape(P, H * P).astype(np.float32),
        "experts1": by_partition(transposed(a["L1_ffn_W_experts"])),
        "router1": transposed(a["L1_ffn_W_router"]), "brouter1": a["L1_ffn_b_router"], "bexp1": a["L1_ffn_b_experts"],
        "iota8": np.arange(EXPERTS1, dtype=np.float32),
    })
    nc = bacc.Bacc("TRN2", target_bir_lowering=False, num_devices=1)
    arrays = {"in_" + n: np.ascontiguousarray(w) for n, w in arrays.items()}
    t = {n[3:]: nc.dram_tensor(n, w.shape, mybir.dt.from_np(w.dtype), kind="ExternalInput").ap()
         for n, w in arrays.items()}
    t["out"] = nc.dram_tensor("out", (B * S, D), F32, kind="ExternalOutput").ap()
    build(nc, t)
    r = run_bass_kernel_spmd(nc, [arrays], core_ids=[0])
    return r.results[0]["out"].reshape(B, S, D)
```

```python
from contextlib import ExitStack, contextmanager

import concourse.bass as bass
from concourse import mybir

F32 = mybir.dt.float32
BF16 = mybir.dt.bfloat16
I32 = mybir.dt.int32
U32 = mybir.dt.uint32
U8 = mybir.dt.uint8
ALU = mybir.AluOpType
ACT = mybir.ActivationFunctionType
AX = mybir.AxisListType

P = 128
B, S, D = 32, 32, 512
TILES = B * S // P
SEQS = P // S
KD = D // P
NCTX = 257
TAIL = NCTX - S
H = 16
DH = 64
HD = H * DH
BANK = 512
EXPERTS, TOPK, CAP, INTER = 64, 8, 128, 384
EXPERTS1, TOPK1 = 8, 2
SLOTS = 4
ROUND = 8
EW = KD * INTER * 2 + INTER // P * D
MASKED = -1e30
APART = -3e38
EPS = 1e-5
INFO = 6
NOWHERE = 4096
UNSEEN = 1024


class Count:

    def __init__(self):
        self.n, self.i, self.per = 0, None, 0

    def add(self, k=1):
        self.n += k

    def value(self, back=0):
        n = self.n - back
        return n if self.i is None else self.i * self.per + n


@contextmanager
def rounds(eng, n, per):
    starts = [c.n for c, _ in per]
    with eng.Fori(0, n) as i:
        for c, k in per:
            c.i, c.per = i, k
        yield i
    for (c, k), start in zip(per, starts):
        assert c.n == start + k, (c.n - start, k)
        c.i, c.per, c.n = None, 0, start + k * n


def wait(eng, sem, value):
    if not isinstance(value, int) or value > 0:
        eng.wait_ge(sem, value)


class Counts:

    def __init__(self):
        self.xn, self.proj, self.tp, self.p, self.sm = Count(), Count(), Count(), Count(), Count()
        self.s, self.o, self.rest, self.ctxh = Count(), Count(), Count(), Count()
        self.gate, self.sel, self.wmat, self.route = Count(), Count(), Count(), Count()
        self.tail = [Count(), Count()]
        self.ctxT, self.ctxr, self.vlast = [Count(), Count()], [Count(), Count()], Count()


class Attention:

    def __init__(self, name, dh, loads, cross=False, gated=False, rope=False):
        self.name, self.dh, self.loads = name, dh, loads
        self.cross, self.gated, self.rope = cross, gated, rope
        self.width = H * dh
        self.halves = self.width // BANK
        self.chunks = self.width // P
        self.parts = 3 - self.halves
        self.early = [(w, h) for w in "qk" for h in range(self.halves)]
        kinds = ["v"] + ["rest"] * cross + ["gate"] * gated
        self.late = [(w, h) for w in kinds for h in range(self.halves)]
        self.rows = P // dh
        self.places = [c * self.rows + r for r in range(self.rows) for c in range(H // self.rows)]
        self.order = [0, 2, 1, 3] if self.rows == 2 else [0, 1, 2, 3]
        self.per_proj = self.parts + len(self.early) + len(self.late) + 1
        self.per_tp = 4 + 2 * self.halves + 2


def build(nc, t):
    with ExitStack() as ctx:
        def sb(name, words, dt=F32):
            return ctx.enter_context(nc.sbuf_tensor(name, [P, words], dt))[:, :]

        def sem(name):
            return ctx.enter_context(nc.semaphore(name))

        def carve(buf, base, *sizes):
            for n in sizes:
                assert base + n <= buf.shape[1], (base, n)
                yield buf[:, base:base + n]
                base += n

        x = sb("x", TILES * D)
        arena = sb("arena", 33280)
        work = sb("work", 14464)
        small = sb("small", 1240)
        ident = sb("ident", P)
        psum = ctx.enter_context(nc.psum_tensor("psum", [P, 8 * BANK], F32))[:, :]
        bank = [psum[:, n * BANK:(n + 1) * BANK] for n in range(8)]
        PROJ, SCORE, TP = 0, 2, 6

        W = KD * HD
        wq0, wk0, wv0, wo0 = carve(arena, 0, W, W, W, W)
        wgate0, wout0 = carve(arena, 0, W, W)
        wqkv0, bq0, bk0, bv0, bo0 = carve(arena, 17408, 3 * W, HD, HD, HD, D)
        slots = list(carve(arena, 2 * W, *[EW] * SLOTS))
        wk1, wv1, qp, ut = carve(arena, 0, W, W, KD * H * P, KD * H * P)
        wo1, wq1, bo1 = carve(arena, 24576, W, W, D)
        W1 = KD * D
        rope, alibi = carve(arena, 0, 4 * D, H * P)
        awv1, awo1, awq1, awk1 = carve(arena, 24576, W1, W1, W1, W1)
        (wexp1,) = carve(arena, 2 * W, EXPERTS1 * W1)

        xn, xnT = carve(work, 0, D, D)
        (ctxh, q, k, v, gate, qT, kT, s, pT, tail0, tail1, rest) = carve(
            work, 2 * D, D, HD, HD, HD, HD, HD, HD, H * P, H * P, KD * TAIL, KD * TAIL, D)
        tail = [tail0, tail1]
        o, oT = s[:, 0:HD], pT[:, 0:HD]
        vrest = gate

        router0, iota64, tokens, tri, ones = carve(arena, 32768, KD * EXPERTS, EXPERTS, TILES * 3, P // 2, P // 2)
        (logit, prob, sel, ranked, chosen, wsel, wrest, eq, selb, cumb, posm, slotinfo, iota128,
         onehot0, onehot1, xg0, xg1, xgT0, xgT1, gtanh, hid0, hid1, y0, y1,
         stats_all, mv_all, var_all, half_all, root_all, step_all) = carve(
            work, 2 * D, EXPERTS, EXPERTS, EXPERTS, TOPK, TOPK, EXPERTS, EXPERTS, TOPK * EXPERTS,
            EXPERTS // 2, EXPERTS // 2, TILES * EXPERTS, TILES * EXPERTS * INFO // 2, CAP,
            TILES * CAP // 2, TILES * CAP // 2, D, D, D, D, INTER, INTER, INTER, D, D,
            6 * TILES, 2 * TILES, TILES, TILES, TILES, TILES)
        chosen_u = chosen.bitcast(U32)
        selb, cumb, slotinfo, tri, ones = (b.bitcast(BF16) for b in (selb, cumb, slotinfo, tri, ones))
        onehot, xg, xgT = [onehot0.bitcast(BF16), onehot1.bitcast(BF16)], [xg0, xg1], [xgT0, xgT1]
        hid, y = [hid0, hid1], [y0, y1]

        (q1, qT1, o1, p1, pT1, ctxT0, ctxr0, ctxT1, ctxr1, vlast, bq1, bk1, bv1) = carve(
            work, 2 * D, HD, HD, HD, SEQS * NCTX, 2 * SEQS * P, *[KD * NCTX, 2 * D] * 2, HD, HD, HD, HD)
        ctxT, ctxr = [ctxT0, ctxT1], [ctxr0, ctxr1]
        oT1, qk = qT1, o1
        ctx_last = p1[:, 0:KD * B]

        router1, wmat, wT, bexp, brouter, iota8, logit1, prob1, pick, ranked1, chosen1 = carve(
            work, 2 * D, KD * EXPERTS1, P, P, D, *[EXPERTS1] * 7)

        def some(n, at=[0]):
            at[0] += n
            assert at[0] <= 1240, at
            return small[:, at[0] - n:at[0]]

        stats, mv, var, half, root, step = some(6), some(2), some(1), some(1), some(1), some(1)
        negmax, total, inv, restp = some(H), some(H), some(H), some(H)
        blockmask, causal, apart = some(P), some(P), some(P)
        keymask = some(TILES * S)
        keymask_u8 = some(TILES * S // 4)
        csum = some(KD * SEQS)
        top, rsum, rinv = some(1), some(1), some(1)
        gidx, sidx, wslot = carve(keymask_u8, 2 * H, ROUND, ROUND, ROUND)
        fidx, empty, zero, held = some(1), some(1), some(1), some(1)
        ctok, crow, negc = some(H), some(H), some(SEQS)
        ends = restp[:, 0:2 * SEQS]
        tok_ends = keymask_u8[:, 0:2 * H]

        xn_d = nc.dram_tensor("xn_rows", (B * S, D), F32, kind="Internal").ap()
        x_d = nc.dram_tensor("x_rows", (B * S, D), F32, kind="Internal").ap()
        vlast_d = nc.dram_tensor("last_values", (B, HD), F32, kind="Internal").ap()

        s_x0, s_x = sem("x_tile0_loaded"), sem("x_loaded")
        s_ident, s_const = sem("identity_loaded"), sem("constants_loaded")
        s_w = {n: sem("loaded_" + n) for n in ("q0", "k0", "v0", "o0", "bias_qk0", "bias_vo0", "qkv0", "gate0", "out0", "tables0", "iota128",
                                         "k1", "v1", "q1", "o1", "ctx_last", "bias_q1", "bias1", "bo1", "rope", "alibi", "aq1", "ak1", "av1", "ao1",
                                         "tables1", "experts1")}
        s_ctxh, s_tail_used = sem("ctx_head_loaded"), sem("ctx_tail_summed")
        s_tail = [sem("ctx_tail_even_loaded"), sem("ctx_tail_odd_loaded")]
        s_rest = sem("ctx_rest_ready")
        s_ready = sem("small_tables_ready")
        s_xn = sem("xn_ready")
        s_proj, s_proj_free = sem("projection_full"), sem("projection_taken")
        s_tp, s_tp_free = sem("transposed_full"), sem("transposed_taken")
        s_s, s_sm, s_p = sem("scores_full"), sem("scores_masked"), sem("probs_ready")
        s_o, s_o_ready = sem("output_full"), sem("output_ready")
        s_gate, s_gate_tanh = sem("gate_ready"), sem("gate_tanh_ready")
        s_end = {n: sem("finished_" + n) for n in ("xattn0", "attn0", "moe0", "xattn1", "attn1")}
        s_out = sem("stored")
        s_xn_d, s_x_d, s_x_back = sem("xn_rows_written"), sem("x_rows_written"), [sem("x_tile0_back"), sem("x_back")]
        s_logit, s_exp, s_sel = sem("logits_ready"), sem("routing_exp_ready"), sem("choice_ready")
        s_ew = [sem(f"expert_weights_{j}") for j in range(SLOTS)]
        s_onehot, s_idx, s_slot = sem("onehot_ready"), sem("slots_full"), sem("slots_ready")
        s_gather = [sem("gathered_even"), sem("gathered_odd")]
        s_xgt, s_xgt_free = sem("slots_turned"), sem("slots_turned_taken")
        s_g, s_gu, s_gtanh, s_h = sem("gate_full"), sem("up_full"), sem("expert_tanh_ready"), sem("hidden_ready")
        s_y, s_y_ready = sem("down_full"), sem("down_ready")
        s_scatter = sem("scattered")
        s_ctxT = [sem("ctx_columns_even"), sem("ctx_columns_odd")]
        s_ctxr = [sem("ctx_rows_even"), sem("ctx_rows_odd")]
        s_vlast_d, s_vlast = sem("last_values_written"), sem("last_values_loaded")
        s_held = sem("held")
        s_wmat, s_final = sem("expert_shares_ready"), sem("tile_final")

        xattn0 = Attention("xattn0", DH, {"q": "q0", "k": "k0", "v": "v0", "out": "o0"}, cross=True)
        attn0 = Attention("attn0", DH, {"q": "qkv0", "gate": "gate0", "out": "out0"}, gated=True)
        attn1 = Attention("attn1", D // H, {"q": "aq1", "k": "ak1", "v": "av1", "out": "ao1"}, rope=True)
        weights = {(attn1, "q"): awq1, (attn1, "k"): awk1, (attn1, "v"): awv1, (attn1, "out"): awo1, (xattn0, "q"): wq0, (xattn0, "k"): wk0, (xattn0, "v"): wv0, (xattn0, "rest"): wv0,
                   (xattn0, "out"): wo0, (attn0, "gate"): wgate0, (attn0, "out"): wout0}
        for n, which in enumerate("qkv"):
            weights[attn0, which] = wqkv0[:, n * W:(n + 1) * W]

        def moving(st, which, half_):
            w = weights[st, which].rearrange("p (k n) -> p k n", k=KD)
            return w[:, :, half_ * BANK:(half_ + 1) * BANK]

        block = ctx.enter_context(nc.Block())

        ROUTE_PROJ, CROSS_PROJ = 4, 3 + H
        CROSS_TILE = CROSS_PROJ + SEQS * 4 + 3

        def pe_project(pe, c, emit, banks=2):
            wait(pe, s_proj_free, c.proj.value(banks - 1))
            emit(bank[PROJ + c.proj.n % banks]).then_inc(s_proj, 1)
            c.proj.add()

        def pe_transpose(pe, c, pieces):
            wait(pe, s_tp_free, c.tp.value(1))
            to = bank[TP + c.tp.n % 2]
            for j, src in enumerate(pieces):
                done = nc.tensor.transpose(to[:, j * P:(j + 1) * P], src, ident[:, :])
            done.then_inc(s_tp, 1)
            c.tp.add()

        def pe_turn_xn(pe, c, parts, banks=2):
            c.xn.add()
            wait(pe, s_xn, c.xn.value())
            n = KD // parts
            for part in range(parts):
                def emit(to):
                    for j in range(n):
                        at = (part * n + j) * P
                        done = nc.tensor.transpose(to[:, j * P:(j + 1) * P], xn[:, at:at + P], ident[:, :])
                    return done
                pe_project(pe, c, emit, banks)

        def attention_pe(pe, st, c):
            def projections(blocks, first=False):
                for which, half_ in blocks:
                    if first and half_ == 0 and which in st.loads:
                        pe.wait_ge(s_w[st.loads[which]], 16)
                    src = xnT
                    if st.cross and which in "kv":
                        src = ctxh
                    if st.cross and which == "k" and half_ == 0:
                        c.ctxh.add(16)
                        wait(pe, s_ctxh, c.ctxh.value())
                    if which == "rest":
                        src = rest
                        if half_ == 0:
                            c.rest.add()
                            wait(pe, s_rest, c.rest.value())
                    w = moving(st, which, half_)

                    def emit(to):
                        for j in range(KD):
                            done = nc.tensor.matmul(to, src[:, j * P:(j + 1) * P], w[:, j, :],
                                                    start=(j == 0), stop=(j == KD - 1))
                        return done
                    pe_project(pe, c, emit)

            def turn_probs():
                for g in st.order:
                    c.p.add()
                    wait(pe, s_p, c.p.value())
                    pe_transpose(pe, c, [s[:, (4 * g + j) * P:(4 * g + j + 1) * P] for j in range(4)])

            def first_half(first=False):
                pe_turn_xn(pe, c, st.parts)
                if not first:
                    turn_probs()
                wait(pe, s_proj_free, c.proj.value())
                projections(st.early, first)

            def turn_qk():
                wait(pe, s_proj_free, c.proj.value(len(st.late)))
                for src in (q, k):
                    for half_ in range(st.halves):
                        pe_transpose(pe, c, [src[:, (half_ * 4 + j) * P:(half_ * 4 + j + 1) * P] for j in range(4)])
                return c.tp.value()

            def scores(turned):
                wait(pe, s_tp_free, turned)
                for h in range(H):
                    ch, off = divmod(h * st.dh, P)
                    n = st.places.index(h)
                    done = nc.tensor.matmul(bank[SCORE + n // 4][:, n % 4 * P:(n % 4 + 1) * P],
                                            qT[off:off + st.dh, ch * P:(ch + 1) * P],
                                            kT[off:off + st.dh, ch * P:(ch + 1) * P], start=True, stop=True)
                    if n % 4 == 3:
                        done.then_inc(s_s, 1)

            def values():
                for m, g in enumerate(st.order):
                    wait(pe, s_tp_free, c.tp.value(3 - m))
                    for n in range(4 * g, 4 * g + 4):
                        at = st.places[n] * st.dh
                        done = nc.tensor.matmul(bank[SCORE + at // BANK][:, at % BANK:at % BANK + st.dh],
                                                pT[:, n * P:(n + 1) * P], v[:, at:at + st.dh], start=True, stop=True)
                done.then_inc(s_o, 1)

            def turn_out():
                c.o.add()
                wait(pe, s_o_ready, c.o.value())
                n = st.chunks // 2
                for part in range(2):
                    pe_transpose(pe, c, [o[:, (part * n + j) * P:(part * n + j + 1) * P] for j in range(n)])

            def project_out():
                wait(pe, s_tp_free, c.tp.value())
                w = weights[st, "out"].rearrange("p (k n) -> p k n", k=st.chunks)

                def emit(to):
                    for j in range(st.chunks):
                        done = nc.tensor.matmul(to, oT[:, j * P:(j + 1) * P], w[:, j, :],
                                                start=(j == 0), stop=(j == st.chunks - 1))
                    return done
                pe_project(pe, c, emit)

            first_half(True)
            wait(pe, s_proj_free, c.proj.value(1))
            projections(st.late, True)
            scores(turn_qk())
            pe.wait_ge(s_w[st.loads["out"]], 16)
            counts = [(c.xn, 1), (c.proj, st.per_proj), (c.tp, st.per_tp), (c.p, 4), (c.o, 1)]
            if st.cross:
                counts += [(c.ctxh, 16), (c.rest, 1)]
            with rounds(pe, TILES - 1, counts):
                first_half()
                values()
                projections(st.late)
                turned = turn_qk()
                turn_out()
                scores(turned)
                project_out()
            turn_probs()
            values()
            turn_out()
            project_out()

        def route_pe(pe, c):
            def tile():
                pe_turn_xn(pe, c, 2)
                wait(pe, s_proj_free, c.proj.value())

                def logits(to):
                    for j in range(KD):
                        done = nc.tensor.matmul(to[:, 0:EXPERTS], xnT[:, j * P:(j + 1) * P],
                                                router0[:, j * EXPERTS:(j + 1) * EXPERTS], start=(j == 0), stop=(j == KD - 1))
                    return done

                def positions(to):
                    nc.tensor.matmul(to[:, 0:EXPERTS], tri, selb, start=True, stop=False)
                    return nc.tensor.matmul(to[:, 0:EXPERTS], ones, cumb, start=False, stop=True)
                pe_project(pe, c, logits)
                c.sel.add()
                wait(pe, s_sel, c.sel.value())
                pe_project(pe, c, positions)

            pe.wait_ge(s_w["tables0"], 16 * TABLES0)
            tile()
            with rounds(pe, TILES - 1, [(c.xn, 1), (c.proj, ROUTE_PROJ), (c.sel, 1)]):
                tile()

        def experts_pe(pe, c):
            def slots_of(e, r):
                wait(pe, s_onehot, ROUND * r + e + 1)
                wait(pe, s_slot, ROUND * r + e)
                info = slotinfo.rearrange("p (t e n) -> p t e n", t=TILES, e=EXPERTS)
                for j in range(TILES):
                    at = ROUND * r + e
                    if isinstance(at, int):
                        rhs = info[:, j, at, :]
                    else:
                        rhs = slotinfo[:, bass.ds(at * INFO + j * EXPERTS * INFO, INFO)]
                    done = nc.tensor.matmul(bank[7][:, 0:INFO], onehot[e % 2][:, j * CAP:(j + 1) * CAP], rhs,
                                            start=(j == 0), stop=(j == TILES - 1))
                done.then_inc(s_idx, 1)

            def turn(e, r):
                wait(pe, s_gather[e % 2], 64 * r + 16 * (e // 2) + 16)
                wait(pe, s_xgt_free, ROUND * r + e)
                for j in range(KD):
                    done = nc.tensor.transpose(bank[4][:, j * P:(j + 1) * P], xg[e % 2][:, j * P:(j + 1) * P], ident)
                done.then_inc(s_xgt, 1)

            def gate_up(e, r):
                wait(pe, s_ew[e % SLOTS], 32 * r + 16 * (e // SLOTS) + 16)
                wait(pe, s_xgt_free, ROUND * r + e + 1)
                for m in range(2):
                    w = slots[e % SLOTS][:, m * KD * INTER:(m + 1) * KD * INTER]
                    to = bank[e % 2 * 2 + m]
                    for n in range(INTER // P):
                        for j in range(KD):
                            at = j * INTER + n * P
                            done = nc.tensor.matmul(to[:, n * P:(n + 1) * P], w[:, at:at + P],
                                                    xgT[e % 2][:, j * P:(j + 1) * P], start=(j == 0), stop=(j == KD - 1))
                    done.then_inc([s_g, s_gu][m], 1)

            def down(e, r):
                wait(pe, s_h, ROUND * r + e + 1)
                w = slots[e % SLOTS][:, 2 * KD * INTER:]
                for j in range(INTER // P):
                    done = nc.tensor.matmul(bank[5 + e % 2], hid[e % 2][:, j * P:(j + 1) * P], w[:, j * D:(j + 1) * D],
                                            start=(j == 0), stop=(j == INTER // P - 1))
                done.then_inc(s_y, 1)

            for e in range(4):
                slots_of(e, 0)
            turn(0, 0)
            gate_up(0, 0)
            turn(1, 0)

            def eight(r, final):
                for e in range(ROUND):
                    if not (final and e >= ROUND - 1):
                        gate_up(e + 1, r)
                    if not (final and e >= ROUND - 2):
                        turn(e + 2, r)
                    if not (final and e >= ROUND - 4):
                        slots_of(e + 4, r)
                    down(e, r)
            with pe.Fori(0, EXPERTS // ROUND - 1) as r:
                eight(r, False)
            eight(EXPERTS // ROUND - 1, True)

        def cross_pe(pe, c):
            qpv = qp.rearrange("p (c b n) -> p c b n", c=KD, b=SEQS)
            utv = ut.rearrange("p (c h n) -> p c h n", c=KD, h=H)

            def project_q(behind):
                wait(pe, s_proj_free, c.proj.value(behind))
                w = wq1.rearrange("p (k n) -> p k n", k=KD)
                for half_ in range(2):
                    def emit(to):
                        for j in range(KD):
                            done = nc.tensor.matmul(to, xnT[:, j * P:(j + 1) * P], w[:, j, half_ * BANK:(half_ + 1) * BANK],
                                                    start=(j == 0), stop=(j == KD - 1))
                        return done
                    pe_project(pe, c, emit)

            def turn_q():
                for half_ in range(2):
                    wait(pe, s_proj_free, c.proj.value(1 - half_))
                    pe_transpose(pe, c, [q1[:, (half_ * 4 + j) * P:(half_ * 4 + j + 1) * P] for j in range(4)])

            def queries_wk():
                for h in range(H):
                    if h % 8 == 0:
                        wait(pe, s_tp_free, c.tp.value(1 - h // 8))
                    pair, off = h // 2, h % 2 * DH

                    def emit(to):
                        for j in range(KD):
                            at = pair * D + j * P
                            done = nc.tensor.matmul(to[:, j * P:(j + 1) * P], wk1[off:off + DH, at:at + P],
                                                    qT1[off:off + DH, pair * P:(pair + 1) * P], start=True, stop=True)
                        return done
                    pe_project(pe, c, emit)

            def last_values():
                w = wv1.rearrange("p (k n) -> p k n", k=KD)
                for half_ in range(2):
                    def emit(to):
                        for j in range(KD):
                            done = nc.tensor.matmul(to[0:B, :], ctx_last[:, j * B:(j + 1) * B],
                                                    w[:, j, half_ * BANK:(half_ + 1) * BANK], start=(j == 0), stop=(j == KD - 1))
                        return done
                    pe_project(pe, c, emit)

            def scores(b):
                c.ctxT[b % 2].add(16)
                wait(pe, s_ctxT[b % 2], c.ctxT[b % 2].value())
                for rt in range(4):
                    for j in range(KD):
                        done = nc.tensor.matmul(bank[SCORE + rt][:, 0:NCTX], qpv[:, j, b, rt * P:(rt + 1) * P],
                                                ctxT[b % 2][:, j * NCTX:(j + 1) * NCTX], start=(j == 0), stop=(j == KD - 1))
                    done.then_inc(s_s, 1)

            def turn_weights():
                c.p.add(4)
                wait(pe, s_p, c.p.value())
                for kc in range(2):
                    pe_transpose(pe, c, [p1[:, rt * NCTX + kc * P:rt * NCTX + (kc + 1) * P] for rt in range(4)])

            def mix(b):
                c.ctxr[b % 2].add(16)
                wait(pe, s_ctxr[b % 2], c.ctxr[b % 2].value())
                wait(pe, s_tp_free, c.tp.value())
                for j in range(KD):
                    def emit(to):
                        for kc in range(2):
                            at = kc * D + j * P
                            done = nc.tensor.matmul(to, ctxr[b % 2][:, at:at + P], pT1[:, kc * 4 * P:(kc + 1) * 4 * P],
                                                    start=(kc == 0), stop=(kc == 1))
                        return done
                    pe_project(pe, c, emit)

            def out_heads(half_):
                w = wv1.rearrange("p (k n) -> p k n", k=KD)

                def emit(to):
                    for h in range(half_ * 8, half_ * 8 + 8):
                        for j in range(KD):
                            done = nc.tensor.matmul(to[:, h % 8 * DH:(h % 8 + 1) * DH], utv[:, j, h, :],
                                                    w[:, j, h * DH:(h + 1) * DH], start=(j == 0), stop=(j == KD - 1))
                    return done
                pe_project(pe, c, emit)

            def turn_out():
                for half_ in range(2):
                    wait(pe, s_proj_free, c.proj.value(1 - half_))
                    pe_transpose(pe, c, [o1[:, (half_ * 4 + j) * P:(half_ * 4 + j + 1) * P] for j in range(4)])

            def project_out():
                w = wo1.rearrange("p (k n) -> p k n", k=HD // P)

                def emit(to):
                    for j in range(HD // P):
                        if j % 4 == 0:
                            wait(pe, s_tp_free, c.tp.value(1 - j // 4))
                        done = nc.tensor.matmul(to, oT1[:, j * P:(j + 1) * P], w[:, j, :],
                                                start=(j == 0), stop=(j == HD // P - 1))
                    return done
                pe_project(pe, c, emit)

            def tile(final):
                for b in range(SEQS - 1):
                    turn_weights()
                    scores(b + 1)
                    mix(b)
                turn_weights()
                if not final:
                    pe_turn_xn(pe, c, 1)
                mix(SEQS - 1)
                if not final:
                    project_q(KD)
                    turn_q()
                    queries_wk()
                wait(pe, s_proj_free, c.proj.value(0 if final else 2 + H))
                out_heads(0)
                if not final:
                    wait(pe, s_proj_free, c.proj.value(1))
                    scores(0)
                out_heads(1)
                turn_out()
                project_out()

            for name in ("q1", "k1", "v1"):
                pe.wait_ge(s_w[name], 16)
            pe_turn_xn(pe, c, 1)
            project_q(0)
            turn_q()
            queries_wk()
            pe.wait_ge(s_w["ctx_last"], 16)
            last_values()
            wait(pe, s_proj_free, c.proj.value(2))
            scores(0)
            pe.wait_ge(s_w["o1"], 16)
            with rounds(pe, TILES - 1, [(c.xn, 1), (c.proj, CROSS_TILE), (c.tp, 4 + 2 * SEQS), (c.p, 4 * SEQS),
                                        *[(n, 16 * SEQS // 2) for n in c.ctxT + c.ctxr]]):
                tile(False)
            tile(True)

        def moe1_pe(pe, c):
            pe.wait_ge(s_w["experts1"], 16 * EXPERTS1)
            pe.wait_ge(s_w["tables1"], 16 * TABLES1)
            wait(pe, s_proj_free, c.proj.value())

            def tile():
                pe_turn_xn(pe, c, 2, 4)
                wait(pe, s_proj_free, c.proj.value())

                def product(w, n):
                    def emit(to):
                        for j in range(KD):
                            done = nc.tensor.matmul(to[:, 0:n], xnT[:, j * P:(j + 1) * P], w[:, j * n:(j + 1) * n],
                                                    start=(j == 0), stop=(j == KD - 1))
                        return done
                    pe_project(pe, c, emit, 4)
                product(router1, EXPERTS1)
                for e in range(EXPERTS1):
                    product(wexp1[:, e * W1:(e + 1) * W1], D)
                c.wmat.add()
                wait(pe, s_wmat, c.wmat.value())
                pe_transpose(pe, c, [wmat])
                wait(pe, s_tp_free, c.tp.value())
                pe_project(pe, c, lambda to: nc.tensor.matmul(to, wT[0:EXPERTS1, :], bexp[0:EXPERTS1, :],
                                                              start=True, stop=True), 4)
            with rounds(pe, TILES // 2, [(c.xn, 2), (c.proj, 24), (c.tp, 2), (c.wmat, 2)]):
                tile()
                tile()

        def inverse_roots(dve, var, half, root, step):
            nc.vector.tensor_single_scalar(half.bitcast(I32), var.bitcast(I32), 1, ALU.logical_shift_right)
            dve.drain()
            nc.vector.tensor_scalar(root.bitcast(I32), half.bitcast(I32), -1.0, float(0x5F3759DF), ALU.mult, ALU.add)
            for _ in range(3):
                dve.drain()
                if var.free_size() == 1:
                    nc.vector.scalar_tensor_tensor(step, root, var, root, ALU.mult, ALU.mult)
                else:
                    nc.vector.tensor_tensor(step, root, var, ALU.mult)
                    dve.drain()
                    nc.vector.tensor_tensor(step, step, root, ALU.mult)
                dve.drain()
                nc.vector.tensor_scalar(step, step, -0.5, 1.5, ALU.mult, ALU.add)
                dve.drain()
                nc.vector.tensor_tensor(root, root, step, ALU.mult)
            dve.drain()

        def layernorm(dve, i):
            xt = x[:, bass.ds(i * D, D)]
            dve.drain()
            nc.vector.bn_stats(stats, xt)
            dve.drain()
            nc.vector.bn_aggr(mv, stats)
            dve.drain()
            nc.vector.tensor_scalar(var, mv[:, 1:2], EPS, None, ALU.add)
            dve.drain()
            inverse_roots(dve, var, half, root, step)
            nc.vector.tensor_scalar(xn, xt, mv[:, 0:1], root, ALU.subtract, ALU.mult).then_inc(s_xn, 1)

        def statistics(dve):
            dve.drain()
            for j in range(1, TILES):
                nc.vector.bn_stats(stats_all[:, 6 * j:6 * j + 6], x[:, j * D:(j + 1) * D])
            dve.drain()
            for j in range(1, TILES):
                nc.vector.bn_aggr(mv_all[:, 2 * j:2 * j + 2], stats_all[:, 6 * j:6 * j + 6])
            dve.drain()
            nc.vector.tensor_scalar(var_all[:, 1:], mv_all[:, 3::2], EPS, None, ALU.add)
            dve.drain()
            inverse_roots(dve, var_all[:, 1:], half_all[:, 1:], root_all[:, 1:], step_all[:, 1:])

        def dve_take(dve, c, op, banks=2):
            c.proj.add()
            wait(dve, s_proj, c.proj.value())
            op(bank[PROJ + (c.proj.n - 1) % banks]).then_inc(s_proj_free, 1)

        def dve_take_xn(dve, c, parts, banks=2):
            n = D // parts
            for part in range(parts):
                dve_take(dve, c, lambda src: nc.vector.tensor_copy(xnT[:, part * n:(part + 1) * n], src[:, 0:n]), banks)

        def heads(st, ap):
            return ap.rearrange("p (r c) -> p c r", r=st.rows).unsqueeze(3).broadcast_to(
                [P, H // st.rows, st.rows, st.dh])

        def by_head(st, ap):
            return ap.rearrange("p (c r n) -> p c r n", r=st.rows, n=st.dh)

        def attention_dve(dve, st, c):
            def take(blocks, then=lambda n: None):
                for n, (which, half_) in enumerate(blocks):
                    part = slice(half_ * BANK, (half_ + 1) * BANK)

                    def op(src):
                        if which in "qk" and st.rope:
                            to, at = {"q": (q, 0), "k": (k, 2 * D)}[which]
                            cos, sin = rope[:, at:at + D], rope[:, at + D:at + 2 * D]
                            swapped = gate[:, 0:D] if which == "q" else gate[:, D:2 * D]
                            turned = swapped.rearrange("p (n two) -> p n two", two=2)
                            pairs, sins = (a.rearrange("p (n two) -> p n two", two=2) for a in (src, sin))
                            nc.vector.tensor_tensor(to[:, part], src, cos, ALU.mult)
                            for n in range(2):
                                nc.vector.tensor_tensor(turned[:, :, n], pairs[:, :, 1 - n], sins[:, :, n], ALU.mult)
                            dve.drain()
                            return nc.vector.tensor_tensor(to[:, part], to[:, part], swapped, ALU.add)
                        if which == "q":
                            if st.cross:
                                return nc.vector.scalar_tensor_tensor(q[:, part], src, st.dh ** -0.5, bq0[:, part],
                                                                      ALU.mult, ALU.add)
                            return nc.vector.tensor_scalar(q[:, part], src, st.dh ** -0.5, None, ALU.mult)
                        if which == "gate":
                            return nc.vector.tensor_copy(gate[:, part], src)
                        if which == "rest":
                            return nc.vector.scalar_tensor_tensor(vrest[:, part], bv0[:, part], float(TAIL), src,
                                                                  ALU.mult, ALU.add)
                        to = {"k": k, "v": v}[which]
                        if st.cross:
                            return nc.vector.tensor_tensor(to[:, part], src, {"k": bk0, "v": bv0}[which][:, part], ALU.add)
                        return nc.vector.tensor_copy(to[:, part], src)
                    dve_take(dve, c, op)
                    then(n)
                if blocks is st.late and st.gated:
                    dve.drain()
                    nc.vector.tensor_copy(step, step).then_inc(s_gate, 1)

            def sum_tail(b):
                c.tail[b % 2].add(16)
                wait(dve, s_tail[b % 2], c.tail[b % 2].value())
                nc.vector.tensor_reduce(csum[:, b:KD * SEQS:SEQS], tail[b % 2].rearrange("p (k n) -> p k n", k=KD),
                                        AX.X, ALU.add).then_inc(s_tail_used, 1)
                if b == SEQS - 1:
                    dve.drain()
                    nc.vector.tensor_copy(rest.rearrange("p (c n) -> p c n", n=S),
                                          csum.unsqueeze(2).broadcast_to([P, KD * SEQS, S])).then_inc(s_rest, 1)

            def take_early():
                take(st.early, sum_tail if st.cross else lambda n: None)

            def mask_scores(i):
                if st.cross:
                    km = keymask[:, bass.ds(i * S, S)]
                    nc.vector.tensor_tensor(blockmask.rearrange("p (b n) -> p b n", b=SEQS),
                                            causal.rearrange("p (b n) -> p b n", b=SEQS),
                                            km.unsqueeze(1).broadcast_to([P, SEQS, S]), ALU.min)
                    dve.drain()
                for m, g in enumerate(st.order):
                    c.s.add()
                    wait(dve, s_s, c.s.value())
                    part = s[:, 4 * g * P:4 * (g + 1) * P].rearrange("p (h n) -> p h n", h=4)
                    if st.rope:
                        mask = alibi[:, 4 * g * P:4 * (g + 1) * P].rearrange("p (h n) -> p h n", h=4)
                    else:
                        mask = (blockmask if st.cross else apart).unsqueeze(1).broadcast_to([P, 4, P])
                    nc.vector.tensor_tensor(part, bank[SCORE + g].rearrange("p (h n) -> p h n", h=4), mask, ALU.add)
                    dve.drain()
                    done = nc.vector.tensor_reduce(negmax[:, 4 * g:4 * g + 4], part, AX.X, ALU.max, negate=True)
                    if m == 3 and st.cross:
                        dve.drain()
                        done = nc.vector.tensor_scalar(restp, negmax, MASKED, None, ALU.add)
                    done.then_inc(s_sm, 1)

            def take_out():
                c.p.add(4)
                wait(dve, s_p, c.p.value())
                if st.cross:
                    nc.vector.scalar_tensor_tensor(total, restp, float(TAIL), total, ALU.mult, ALU.add)
                    dve.drain()
                nc.vector.reciprocal(inv, total)
                dve.drain()
                of = heads(st, inv)
                ov = by_head(st, o[:, 0:st.width])
                src = by_head(st, psum[:, SCORE * BANK:SCORE * BANK + st.width])
                if st.cross:
                    nc.vector.tensor_tensor(restp, restp, inv, ALU.mult)
                    dve.drain()
                    vr = by_head(st, vrest)
                    nc.vector.tensor_tensor(vr, vr, heads(st, restp), ALU.mult)
                if st.gated:
                    c.gate.add()
                    wait(dve, s_gate_tanh, c.gate.value())
                    nc.vector.tensor_scalar(gate, gate, 1.0, 0.5, ALU.add, ALU.mult)
                    dve.drain()
                    gv = by_head(st, gate)
                    nc.vector.tensor_tensor(gv, gv, of, ALU.mult)
                    dve.drain()
                    of = gv
                c.o.add()
                wait(dve, s_o, c.o.value())
                done = nc.vector.tensor_tensor(ov, src, of, ALU.mult)
                if st.cross:
                    dve.drain()
                    done = nc.vector.tensor_tensor(o, o, vrest, ALU.add)
                done.then_inc(s_o_ready, 1)

            def add_to_x(i):
                xt = x[:, bass.ds(i * D, D)]
                dve_take(dve, c, lambda src: nc.vector.tensor_tensor(xt, xt, src, ALU.add))
                if st.cross:
                    dve.drain()
                    nc.vector.tensor_tensor(xt, xt, bo0, ALU.add)

            if st.rope:
                dve.wait_ge(s_w["rope"], 16)
                dve.wait_ge(s_w["alibi"], 16)
            dve_take_xn(dve, c, st.parts)
            if st.cross:
                dve.wait_ge(s_w["bias_qk0"], 16 * 2)
                nc.vector.tensor_scalar(bq0, bq0, DH ** -0.5, None, ALU.mult)
                dve.drain()
            take_early()
            if st.cross:
                dve.wait_ge(s_w["bias_vo0"], 16 * 2)
            take(st.late)
            if st.cross:
                dve.wait_ge(s_const, 16 * 3)
                nc.vector.tensor_scalar(keymask, keymask_u8.bitcast(U8), MASKED, None, ALU.mult)
                dve.wait_ge(s_x, 16)
            layernorm(dve, 1)
            mask_scores(0)
            counts = [(c.proj, st.per_proj), (c.s, 4), (c.p, 4), (c.o, 1)]
            if st.cross:
                counts += [(n, 16 * SEQS // 2) for n in c.tail]
            if st.gated:
                counts += [(c.gate, 1)]
            with rounds(dve, TILES - 1, counts) as i:
                dve_take_xn(dve, c, st.parts)
                take_early()
                take_out()
                take(st.late)
                layernorm(dve, (i + 2) % TILES)
                mask_scores(i + 1)
                add_to_x(i)
            take_out()
            add_to_x(TILES - 1)
            dve.drain()
            nc.vector.tensor_copy(step, step).then_inc(s_end[st.name], 1)

        def route_dve(dve, c):
            def normalise(i):
                xt = x[:, bass.ds(i * D, D)]
                wait(dve, s_xn_d, i * 16)
                nc.vector.tensor_scalar(xn, xt, mv_all[:, bass.ds(i * 2, 1)], root_all[:, bass.ds(i, 1)],
                                        ALU.subtract, ALU.mult).then_inc(s_xn, 1)

            def choose(i, meanwhile=lambda: None):
                dve_take_xn(dve, c, 2)
                dve_take(dve, c, lambda src: nc.vector.tensor_copy(logit, src[:, 0:EXPERTS]))
                dve.drain()
                nc.vector.tensor_reduce(top, logit, AX.X, ALU.max, negate=True).then_inc(s_logit, 1)
                meanwhile()
                c.route.add()
                wait(dve, s_exp, c.route.value())
                nc.vector.reciprocal(rinv, rsum)
                dve.drain()
                nc.vector.tensor_scalar(prob, prob, rinv, None, ALU.mult)
                dve.drain()
                nc.vector.max(ranked, prob)
                dve.drain()
                nc.vector.max_index(chosen_u, ranked, prob)
                nc.vector.tensor_reduce(rsum, ranked, AX.X, ALU.add)
                dve.drain()
                nc.vector.tensor_copy(wrest[:, 0:TOPK], chosen_u)
                nc.vector.reciprocal(rinv, rsum)
                dve.drain()
                eqv = eq.rearrange("p (r e) -> p r e", r=TOPK)
                nc.vector.tensor_tensor(eqv, iota64.unsqueeze(1).broadcast_to([P, TOPK, EXPERTS]),
                                        wrest[:, 0:TOPK].unsqueeze(2).broadcast_to([P, TOPK, EXPERTS]), ALU.is_equal)
                dve.drain()
                nc.vector.tensor_reduce(sel, eq.rearrange("p (r e) -> p e r", r=TOPK), AX.X, ALU.add)
                dve.drain()
                nc.vector.tensor_copy(selb, sel).then_inc(s_sel, 1)
                nc.vector.scalar_tensor_tensor(wsel, prob, rinv, sel, ALU.mult, ALU.mult)
                info = slotinfo[:, bass.ds(i * EXPERTS * INFO, EXPERTS * INFO)].rearrange("p (e n) -> p e n", n=INFO)
                for n in range(3):
                    dve.drain()
                    nc.vector.tensor_copy(info[:, :, 3 + n], wsel)
                    if n < 2:
                        dve.drain()
                        nc.vector.tensor_tensor(wsel, wsel, info[:, :, 3 + n], ALU.subtract)
                nc.vector.tensor_scalar(sel, sel, -float(UNSEEN), float(UNSEEN), ALU.mult, ALU.add)
                dve.drain()
                dve_take(dve, c, lambda src: nc.vector.tensor_tensor(posm[:, bass.ds(i * EXPERTS, EXPERTS)], src[:, 0:EXPERTS],
                                                                     sel, ALU.add))
                nc.vector.tensor_tensor(cumb, cumb, selb, ALU.add)

            dve.wait_ge(s_w["tables0"], 16 * TABLES0)
            nc.vector.memset(cumb, 0.0)
            infov = slotinfo.rearrange("p (t e n) -> p t e n", t=TILES, e=EXPERTS)
            for j in range(TILES):
                nc.vector.tensor_copy(infov[:, j, :, 0:3], tokens[:, 3 * j:3 * j + 3].unsqueeze(1).broadcast_to([P, EXPERTS, 3]))
            statistics(dve)
            with rounds(dve, TILES - 1, [(c.proj, ROUTE_PROJ), (c.route, 1)]) as i:
                choose(i, lambda: normalise(i + 1))
            choose(TILES - 1)
            dve.drain()

        def experts_dve(dve, c):
            posv = posm.rearrange("p (t e) -> p t e", t=TILES)

            def ask(e, r):
                wait(dve, s_idx, ROUND * r + e - 1)
                at = ROUND * r + e
                if isinstance(at, int):
                    place = posv[:, :, at:at + 1]
                else:
                    place = posm[:, bass.ds(at, (TILES - 1) * EXPERTS + 1)][:, 0::EXPERTS].unsqueeze(2)
                nc.vector.tensor_tensor(onehot[e % 2].rearrange("p (t n) -> p t n", t=TILES),
                                        iota128.unsqueeze(1).broadcast_to([P, TILES, CAP]),
                                        place.broadcast_to([P, TILES, CAP]), ALU.is_equal).then_inc(s_onehot, 1)

            def answer(e, r):
                n = e % ROUND
                wait(dve, s_scatter, 128 * r + 16 * (e - ROUND) + 16)
                wait(dve, s_idx, ROUND * r + e + 1)
                src = bank[7]
                nc.vector.tensor_copy(fidx, src[:, 0:1])
                nc.vector.tensor_scalar(empty, src[:, 2:3], -float(NOWHERE), float(NOWHERE), ALU.mult, ALU.add)
                nc.vector.tensor_copy(wslot[:, n:n + 1], src[:, 3:4])
                dve.drain()
                nc.vector.scalar_tensor_tensor(fidx, src[:, 1:2], float(P), fidx, ALU.mult, ALU.add)
                nc.vector.tensor_tensor(wslot[:, n:n + 1], src[:, 4:5], wslot[:, n:n + 1], ALU.add)
                dve.drain()
                nc.vector.tensor_copy(gidx.bitcast(U32)[:, n:n + 1], fidx)
                nc.vector.tensor_tensor(sidx.bitcast(U32)[:, n:n + 1], fidx, empty, ALU.add)
                nc.vector.tensor_tensor(wslot[:, n:n + 1], src[:, 5:6], wslot[:, n:n + 1], ALU.add).then_inc(s_slot, 1)

            def silu_up(e, r):
                wait(dve, s_gtanh, ROUND * r + e + 1)
                nc.vector.scalar_tensor_tensor(gtanh, gtanh, 1.0, bank[e % 2 * 2][:, 0:INTER], ALU.add, ALU.mult)
                dve.drain()
                wait(dve, s_gu, ROUND * r + e + 1)
                nc.vector.scalar_tensor_tensor(hid[e % 2], gtanh, 0.5, bank[e % 2 * 2 + 1][:, 0:INTER],
                                               ALU.mult, ALU.mult).then_inc(s_h, 1)

            def take_down(e, r):
                wait(dve, s_scatter, 128 * r + 16 * (e - 2) + 16)
                wait(dve, s_y, ROUND * r + e + 1)
                nc.vector.tensor_scalar(y[e % 2], bank[5 + e % 2], wslot[:, e % ROUND:e % ROUND + 1], None,
                                        ALU.mult).then_inc(s_y_ready, 1)

            dve.wait_ge(s_w["iota128"], 16)
            for e in range(4):
                ask(e, 0)
                answer(e, 0)

            def eight(r, final):
                for e in range(ROUND):
                    silu_up(e, r)
                    if not (final and e >= ROUND - 4):
                        ask(e + 4, r)
                        answer(e + 4, r)
                    take_down(e, r)
            eight(0, False)
            with dve.Fori(1, EXPERTS // ROUND - 1) as r:
                eight(r, False)
            eight(EXPERTS // ROUND - 1, True)

        def cross_dve(dve, c):
            qpv = qp.rearrange("p (c b h n) -> p c b h n", c=KD, b=SEQS, h=H)
            utv = ut.rearrange("p (c h b n) -> p c h b n", c=KD, h=H, b=SEQS)

            def take_q():
                for half_ in range(2):
                    part = slice(half_ * BANK, (half_ + 1) * BANK)
                    dve_take(dve, c, lambda src: nc.vector.scalar_tensor_tensor(
                        q1[:, part], src, DH ** -0.5, bq1[:, part], ALU.mult, ALU.add))

            def keys_bias():
                dve.drain()
                nc.vector.tensor_tensor(qk, q1, bk1, ALU.mult)
                dve.drain()
                nc.vector.tensor_reduce(ctok, qk.rearrange("p (h n) -> p h n", h=H), AX.X, ALU.add)
                dve.drain()
                for b in range(SEQS):
                    for n in range(4):
                        nc.vector.tensor_copy(crow[n * S:(n + 1) * S, b * 4:b * 4 + 4], ctok[b * S:(b + 1) * S, n::4])

            def take_queries():
                for h in range(H):
                    dve_take(dve, c, lambda src: nc.vector.tensor_copy(
                        qpv[:, :, :, h, :], src.rearrange("p (c b n) -> p c b n", c=KD, b=SEQS)))

            def maxima(b):
                for rt in range(4):
                    c.s.add()
                    wait(dve, s_s, c.s.value())
                    nc.vector.tensor_reduce(negmax[:, rt:rt + 1], bank[SCORE + rt][:, 0:NCTX], AX.X, ALU.max, negate=True)
                dve.drain()
                cb = crow[:, b * 4:b * 4 + 4]
                nc.vector.tensor_tensor(negc, negmax[:, 0:4], cb, ALU.subtract)
                dve.drain()
                nc.vector.tensor_tensor(negc, negc, cb, ALU.add).then_inc(s_sm, 1)

            def move_ends(b):
                c.p.add(4)
                wait(dve, s_p, c.p.value())
                nc.vector.tensor_copy(ends[:, SEQS:], p1.rearrange("p (r n) -> p r n", r=4)[:, :, NCTX - 1])
                dve.drain()
                for n in range(4):
                    nc.vector.tensor_copy(tok_ends[b * S:(b + 1) * S, n * 8:n * 8 + 8], ends[n * S:(n + 1) * S, :])

            def take_mix(b):
                for j in range(KD):
                    dve_take(dve, c, lambda src: nc.vector.tensor_copy(
                        utv[:, j, :, b, :], src.rearrange("p (h n) -> p h n", h=H)))

            def last_share():
                sums, last = (tok_ends.rearrange("p (n k r) -> p k r n", n=4, k=2)[:, k] for k in range(2))
                dve.drain()
                nc.vector.reciprocal(inv.rearrange("p (r n) -> p r n", r=4), sums)
                dve.drain()
                nc.vector.tensor_tensor(negmax.rearrange("p (r n) -> p r n", r=4), last,
                                        inv.rearrange("p (r n) -> p r n", r=4), ALU.mult)
                dve.drain()
                c.vlast.add(16)
                wait(dve, s_vlast, c.vlast.value())
                vl = vlast.rearrange("p (h n) -> p h n", h=H)
                nc.vector.tensor_tensor(vl, vl, negmax.unsqueeze(2).broadcast_to([P, H, DH]), ALU.mult)
                dve.drain()
                nc.vector.tensor_tensor(vlast, vlast, bv1, ALU.add)

            def take_heads(half_):
                part = slice(half_ * BANK, (half_ + 1) * BANK)
                weight = inv[:, half_ * 8:half_ * 8 + 8].unsqueeze(2).broadcast_to([P, 8, DH])

                def op(src):
                    nc.vector.tensor_tensor(o1[:, part].rearrange("p (h n) -> p h n", h=8),
                                            src.rearrange("p (h n) -> p h n", h=8), weight, ALU.mult)
                    dve.drain()
                    return nc.vector.tensor_tensor(o1[:, part], o1[:, part], vlast[:, part], ALU.add)
                dve_take(dve, c, op)

            def add_to_x(i):
                xt = x[:, bass.ds(i * D, D)]
                dve_take(dve, c, lambda src: nc.vector.tensor_tensor(xt, xt, src, ALU.add))
                dve.drain()
                nc.vector.tensor_tensor(xt, xt, bo1, ALU.add)

            def tile(i, final):
                for b in range(SEQS - 1):
                    move_ends(b)
                    maxima(b + 1)
                    take_mix(b)
                move_ends(SEQS - 1)
                if not final:
                    dve_take_xn(dve, c, 1)
                take_mix(SEQS - 1)
                if not final:
                    take_q()
                    take_queries()
                    keys_bias()
                last_share()
                take_heads(0)
                if not final:
                    maxima(0)
                take_heads(1)
                if not final:
                    layernorm(dve, (i + 2) % TILES)
                add_to_x(i)

            dve.wait_ge(s_x_back[0], 16)
            layernorm(dve, 0)
            dve.wait_ge(s_w["bias_q1"], 16)
            nc.vector.tensor_scalar(bq1, bq1, DH ** -0.5, None, ALU.mult)
            dve.drain()
            dve_take_xn(dve, c, 1)
            take_q()
            take_queries()
            for half_ in range(2):
                part = slice(half_ * BANK, (half_ + 1) * BANK)
                dve_take(dve, c, lambda src: nc.vector.tensor_copy(vlast[0:B, part], src[0:B, :]))
            dve.wait_ge(s_w["bias1"], 16 * 2)
            keys_bias()
            dve.wait_ge(s_x_back[1], 16)
            layernorm(dve, 1)
            dve.wait_ge(s_w["bo1"], 16)
            maxima(0)
            with rounds(dve, TILES - 1, [(c.proj, CROSS_TILE), (c.s, 4 * SEQS), (c.p, 4 * SEQS), (c.vlast, 16)]) as i:
                tile(i, False)
            tile(TILES - 1, True)
            dve.drain()
            nc.vector.tensor_copy(step, step).then_inc(s_end["xattn1"], 1)

        def moe1_dve(dve, c):
            dve.wait_ge(s_w["tables1"], 16 * TABLES1)
            nc.vector.memset(wmat, 0.0)
            dve.drain()

            def tile(i):
                xt = x[:, bass.ds(i * D, D)]
                dve_take_xn(dve, c, 2, 4)
                dve_take(dve, c, lambda src: nc.vector.tensor_tensor(logit1, src[:, 0:EXPERTS1], brouter, ALU.add), 4)
                dve.drain()
                nc.vector.tensor_reduce(top, logit1, AX.X, ALU.max, negate=True).then_inc(s_logit, 1)
                c.route.add()
                wait(dve, s_exp, c.route.value())
                nc.vector.reciprocal(rinv, rsum)
                dve.drain()
                nc.vector.tensor_scalar(prob1, prob1, rinv, None, ALU.mult)
                dve.drain()
                nc.vector.max(ranked1, prob1)
                dve.drain()
                nc.vector.max_index(chosen1.bitcast(U32), ranked1, prob1)
                dve.drain()
                nc.vector.tensor_copy(logit1, chosen1.bitcast(U32))
                dve.drain()
                wm = wmat[:, 0:EXPERTS1]
                nc.vector.tensor_scalar(wm, iota8, logit1[:, 0:1], ranked1[:, 0:1], ALU.is_equal, ALU.mult)
                nc.vector.tensor_scalar(pick, iota8, logit1[:, 1:2], ranked1[:, 1:2], ALU.is_equal, ALU.mult)
                dve.drain()
                nc.vector.tensor_tensor(wm, wm, pick, ALU.add).then_inc(s_wmat, 1)
                layernorm(dve, (i + 1) % TILES)
                for e in range(EXPERTS1):
                    dve.drain()
                    dve_take(dve, c, lambda src: nc.vector.scalar_tensor_tensor(xt, src, wmat[:, e:e + 1], xt, ALU.mult, ALU.add), 4)
                dve.drain()
                dve_take(dve, c, lambda src: nc.vector.tensor_tensor(xt, xt, src, ALU.add), 4)
                dve.drain()
                nc.vector.tensor_copy(step, step).then_inc(s_final, 1)
            with rounds(dve, TILES // 2, [(c.proj, 24), (c.route, 2)]) as i:
                tile(i * 2)
                tile(i * 2 + 1)

        def act_take(act, c, to):
            c.tp.add()
            wait(act, s_tp, c.tp.value())
            src = bank[TP + (c.tp.n - 1) % 2]
            nc.scalar.copy(to, src[:, 0:to.free_size()]).then_inc(s_tp_free, 1)

        def attention_act(act, st, c):
            def take_qk():
                for to in (qT, kT):
                    for half_ in range(st.halves):
                        act_take(act, c, to[:, half_ * BANK:(half_ + 1) * BANK])

            def exps():
                if st.gated:
                    c.gate.add()
                    wait(act, s_gate, c.gate.value())
                    nc.scalar.activation(gate, gate, ACT.Tanh, scale=0.5).then_inc(s_gate_tanh, 1)
                for m, g in enumerate(st.order):
                    c.sm.add()
                    wait(act, s_sm, c.sm.value())
                    if m == 3 and st.cross:
                        nc.scalar.activation(restp, restp, ACT.Exp)
                    for n in range(4 * g, 4 * g + 4):
                        part = s[:, n * P:(n + 1) * P]
                        done = nc.scalar.activation(part, part, ACT.Exp, bias=negmax[:, n:n + 1],
                                                    accum_out=total[:, n:n + 1])
                    done.then_inc(s_p, 1)

            def take_probs():
                for g in st.order:
                    act_take(act, c, pT[:, 4 * g * P:4 * (g + 1) * P])

            def take_out():
                n = st.width // 2
                for part in range(2):
                    act_take(act, c, oT[:, part * n:(part + 1) * n])

            take_qk()
            exps()
            counts = [(c.tp, st.per_tp), (c.sm, 4)]
            if st.gated:
                counts += [(c.gate, 1)]
            with rounds(act, TILES - 1, counts):
                take_probs()
                take_qk()
                take_out()
                exps()
            take_probs()
            take_out()

        def route_act(act, c):
            with rounds(act, TILES, [(c.route, 1)]) as i:
                act.wait_ge(s_xn, i + 2 * TILES + 1)
                act.dma_start(xn_d[bass.ds(i * P, P), :], xn).then_inc(s_xn_d, 16)
                c.route.add()
                wait(act, s_logit, c.route.value())
                nc.scalar.activation(prob, logit, ACT.Exp, bias=top, accum_out=rsum).then_inc(s_exp, 1)

        def experts_act(act, c):
            def turned(e, r):
                wait(act, s_xgt, ROUND * r + e + 1)
                nc.scalar.copy(xgT[e % 2], bank[4]).then_inc(s_xgt_free, 1)

            def tanh(e, r):
                wait(act, s_h, ROUND * r + e)
                wait(act, s_g, ROUND * r + e + 1)
                nc.scalar.activation(gtanh, bank[e % 2 * 2][:, 0:INTER], ACT.Tanh, scale=0.5).then_inc(s_gtanh, 1)

            turned(0, 0)
            tanh(0, 0)
            turned(1, 0)

            def eight(r, final):
                for e in range(ROUND):
                    if not (final and e >= ROUND - 1):
                        tanh(e + 1, r)
                    if not (final and e >= ROUND - 2):
                        turned(e + 2, r)
            with act.Fori(0, EXPERTS // ROUND - 1) as r:
                eight(r, False)
            eight(EXPERTS // ROUND - 1, True)

        def cross_act(act, c):
            def turned(to):
                for half_ in range(2):
                    act_take(act, c, to[:, half_ * BANK:(half_ + 1) * BANK])

            def exps():
                c.sm.add()
                wait(act, s_sm, c.sm.value())
                for rt in range(4):
                    nc.scalar.activation(p1[:, rt * NCTX:(rt + 1) * NCTX], bank[SCORE + rt][:, 0:NCTX], ACT.Exp,
                                         bias=negc[:, rt:rt + 1], accum_out=ends[:, rt:rt + 1]).then_inc(s_p, 1)

            def tile(final):
                for b in range(SEQS - 1):
                    turned(pT1)
                    exps()
                turned(pT1)
                if not final:
                    turned(qT1)
                if not final:
                    exps()
                turned(oT1)
            turned(qT1)
            exps()
            with rounds(act, TILES - 1, [(c.tp, 4 + 2 * SEQS), (c.sm, SEQS)]):
                tile(False)
            tile(True)

        def moe1_act(act, c):
            def tile():
                c.route.add()
                wait(act, s_logit, c.route.value())
                nc.scalar.activation(prob1, logit1, ACT.Exp, bias=top, accum_out=rsum).then_inc(s_exp, 1)
                act_take(act, c, wT)
            with rounds(act, TILES // 2, [(c.tp, 2), (c.route, 2)]):
                tile()
                tile()

        TABLES0, TABLES1 = 5, 4
        @block.tensor
        def _(pe):
            c = Counts()
            pe.wait_ge(s_ident, 16)
            attention_pe(pe, xattn0, c)
            attention_pe(pe, attn0, c)
            route_pe(pe, c)
            experts_pe(pe, c)
            cross_pe(pe, c)
            attention_pe(pe, attn1, c)
            moe1_pe(pe, c)

        @block.vector
        def _(dve):
            c = Counts()
            dve.wait_ge(s_x0, 16)
            layernorm(dve, 0)
            attention_dve(dve, xattn0, c)
            attention_dve(dve, attn0, c)
            route_dve(dve, c)
            experts_dve(dve, c)
            cross_dve(dve, c)
            attention_dve(dve, attn1, c)
            moe1_dve(dve, c)

        @block.scalar
        def _(act):
            c = Counts()
            attention_act(act, xattn0, c)
            attention_act(act, attn0, c)
            route_act(act, c)
            experts_act(act, c)
            cross_act(act, c)
            attention_act(act, attn1, c)
            moe1_act(act, c)

        @block.gpsimd
        def _(pool):
            def load(to, name, k, s_):
                pool.dma_start(to.rearrange("p (k n) -> p k n", k=k),
                               t[name].rearrange("(k p) n -> p k n", p=P)).then_inc(s_, 16)

            pool.wait_ge(s_end["attn0"], 1)
            pool.dma_start(iota128, t["iota128"]).then_inc(s_w["iota128"], 16)
            pool.dma_start(x_d.rearrange("(t p) d -> p t d", p=P), x.rearrange("p (t d) -> p t d", t=TILES)).then_inc(s_x_d, 16)
            load(wq1, "q1", KD, s_w["q1"])
            load(wk1, "k1", HD // P, s_w["k1"])
            load(wv1, "v1", KD, s_w["v1"])
            pool.wait_ge(s_xn_d, 16 * TILES)
            pool.wait_ge(s_x_d, 16)
            nc.gpsimd.memset(zero, 0.0)
            pool.drain()

            holds = Count()

            def hold():
                wait(pool, s_held, holds.value())
                nc.gpsimd.tensor_tensor(held, zero, zero, ALU.add).then_inc(s_held, 1)
                holds.add()

            def gather(e, r):
                pool.wait_ge(s_slot, ROUND * r + e + 1)
                wait(pool, s_xgt, ROUND * r + e - 1)
                hold()
                pool.indirect_dma_start(xg[e % 2], None, xn_d, bass.IndirectOffsetOnAxis(
                    ap=gidx.bitcast(U32)[:, e % ROUND:e % ROUND + 1], axis=0)).then_inc(s_gather[e % 2], 16)

            def scatter(e, r):
                pool.wait_ge(s_y_ready, ROUND * r + e + 1)
                wait(pool, s_scatter, 128 * r + 16 * e)
                hold()
                pool.indirect_dma_start(x_d, bass.IndirectOffsetOnAxis(
                    ap=sidx.bitcast(U32)[:, e % ROUND:e % ROUND + 1], axis=0), y[e % 2], None,
                    bounds_check=B * S - 1, oob_is_err=False, compute_op=ALU.add).then_inc(s_scatter, 16)

            def eight(r, final):
                for e in range(ROUND):
                    if not (final and e >= ROUND - 3):
                        gather(e + 3, r)
                    scatter(e, r)
            gather(0, 0)
            gather(1, 0)
            gather(2, 0)
            eight(0, False)
            with rounds(pool, EXPERTS // ROUND - 2, [(holds, 2 * ROUND)]) as r:
                eight(r + 1, False)
            eight(EXPERTS // ROUND - 1, True)
            pool.wait_ge(s_scatter, 16 * EXPERTS)

        @block.sync
        def _(sp):
            def load(to, name, k, s_):
                sp.dma_start(to.rearrange("p (k n) -> p k n", k=k),
                             t[name].rearrange("(k p) n -> p k n", p=P)).then_inc(s_, 16)

            def load_row(to, name, s_):
                sp.dma_start(to, t[name].partition_broadcast(P)).then_inc(s_, 16)

            def load_head(i):
                sp.dma_start(ctxh, t["ctx_head"][bass.ds(i * P, P), :]).then_inc(s_ctxh, 16)

            def load_tail(b, i):
                sp.dma_start(tail[b % 2], t["ctx_tail"][bass.ds((i * SEQS + b) * P, P), :]).then_inc(s_tail[b % 2], 16)

            sp.dma_start(x[:, 0:D], t["x"][0:P, :]).then_inc(s_x0, 16)
            sp.dma_start(ident, t["ident"]).then_inc(s_ident, 16)
            load(wq0, "q0", KD, s_w["q0"])
            load_row(bq0, "bq0", s_w["bias_qk0"])
            load_head(0)
            load(wk0, "k0", KD, s_w["k0"])
            load_row(bk0, "bk0", s_w["bias_qk0"])
            load_tail(0, 0)
            load_tail(1, 0)
            load(wv0, "v0", KD, s_w["v0"])
            for to, name in ((bv0, "bv0"), (bo0, "bo0")):
                load_row(to, name, s_w["bias_vo0"])
            for to, name in ((causal, "mask_causal"), (apart, "mask_apart")):
                sp.dma_start(to, t[name]).then_inc(s_const, 16)
            sp.dma_start(keymask_u8.bitcast(U8), t["mask"]).then_inc(s_const, 16)
            sp.dma_start(x[:, D:].rearrange("p (t d) -> p t d", t=TILES - 1),
                         t["x"][P:, :].rearrange("(t p) d -> p t d", p=P)).then_inc(s_x, 16)
            for b in (2, 3):
                sp.wait_ge(s_tail_used, b - 1)
                load_tail(b, 0)
            load(wo0, "o0", H * DH // P, s_w["o0"])

            V_READ = xattn0.parts + len(xattn0.early) + xattn0.halves

            def load_tile(i, projected):
                for b in range(SEQS):
                    if b == 2:
                        sp.wait_ge(s_proj, projected)
                        load_head(i)
                    sp.wait_ge(s_tail_used, i * SEQS + b - 1)
                    load_tail(b, i)
            load_tile(1, V_READ)
            with sp.Fori(2, TILES) as i:
                load_tile(i, (i - 1) * xattn0.per_proj - 1 + V_READ)
            load(wqkv0, "qkv0", 3 * KD, s_w["qkv0"])
            sp.wait_ge(s_proj, TILES * xattn0.per_proj - len(xattn0.late) - 1)
            load(wgate0, "gate0", KD, s_w["gate0"])
            load(wout0, "out0", HD // P, s_w["out0"])
            sp.wait_ge(s_end["xattn0"], 1)
            load(router0, "router0", KD, s_w["tables0"])
            for to, name in ((iota64, "iota64"), (tokens, "tokens"), (tri, "tri"), (ones, "ones")):
                sp.dma_start(to, t[name]).then_inc(s_w["tables0"], 16)
            for j in range(SLOTS):
                if j == 2:
                    sp.wait_ge(s_end["attn0"], 1)
                sp.dma_start(slots[j], t["experts0"][j * P:(j + 1) * P, :]).then_inc(s_ew[j], 16)
            with sp.Fori(1, EXPERTS // SLOTS) as r:
                for j in range(SLOTS):
                    sp.wait_ge(s_y, r * 4 - 3 + j)
                    sp.dma_start(slots[j], t["experts0"][bass.ds((r * SLOTS + j) * P, P), :]).then_inc(s_ew[j], 16)
            sp.wait_ge(s_scatter, 16 * EXPERTS)
            sp.dma_start(x[:, 0:D], x_d[0:P, :]).then_inc(s_x_back[0], 16)
            load_row(bq1, "bq1", s_w["bias_q1"])
            sp.dma_start(ctx_last, t["ctx_last"]).then_inc(s_w["ctx_last"], 16)
            for to, name in ((bk1, "bk1"), (bv1, "bv1")):
                load_row(to, name, s_w["bias1"])

            def load_columns(b, seq):
                sp.dma_start(ctxT[b % 2], t["ctxT"][bass.ds(seq * P, P), :]).then_inc(s_ctxT[b % 2], 16)

            def load_rows(b, seq):
                sp.dma_start(ctxr[b % 2].rearrange("p (c d) -> p c d", c=2),
                             t["ctx"][bass.ds(seq, 1), 0:2 * P, :].rearrange("o (c p) d -> (o p) c d", p=P)).then_inc(s_ctxr[b % 2], 16)

            def load_last(i):
                sp.dma_start(vlast, vlast_d[bass.ds(i * SEQS, SEQS), :].unsqueeze(1).broadcast_to([SEQS, S, HD])).then_inc(s_vlast, 16)

            before = TILES * (xattn0.per_proj + attn0.per_proj + ROUTE_PROJ) + CROSS_PROJ + 2
            mixed = [KD, 2 * KD, 3 * KD, 4 * KD + 1]
            before_s = TILES * 4 * 2

            def load_ctx(b, i):
                if isinstance(i, int) and b < 2:
                    load_columns(b, i * SEQS + b)
                    load_rows(b, i * SEQS + b)
                    return
                sp.wait_ge(s_s, (i * SEQS + b - 1) * 4 + before_s)
                load_columns(b, i * SEQS + b)
                sp.wait_ge(s_proj, i * CROSS_TILE + before + mixed[b - 2] if b >= 2
                           else (i - 1) * CROSS_TILE + before + mixed[b + 2])
                load_rows(b, i * SEQS + b)
            load_ctx(0, 0)
            load_ctx(1, 0)
            sp.dma_start(x[:, D:].rearrange("p (t d) -> p t d", t=TILES - 1),
                         x_d[P:, :].rearrange("(t p) d -> p t d", p=P)).then_inc(s_x_back[1], 16)
            load(wo1, "o1", HD // P, s_w["o1"])
            load_row(bo1, "bo1", s_w["bo1"])
            sp.wait_ge(s_proj_free, before)
            sp.dma_start(vlast_d, vlast[0:B, :]).then_inc(s_vlast_d, 16)
            sp.wait_ge(s_vlast_d, 16)
            load_last(0)
            load_ctx(2, 0)
            load_ctx(3, 0)
            with sp.Fori(1, TILES) as i:
                load_ctx(0, i)
                load_ctx(1, i)
                sp.wait_ge(s_proj_free, i * CROSS_TILE + before - 1)
                load_last(i)
                load_ctx(2, i)
                load_ctx(3, i)
            sp.wait_ge(s_proj, before + (TILES - 1) * CROSS_TILE - 3)
            load(awq1, "aq1", KD, s_w["aq1"])
            load(awk1, "ak1", KD, s_w["ak1"])
            sp.dma_start(rope, t["rope"]).then_inc(s_w["rope"], 16)
            sp.dma_start(alibi, t["alibi"]).then_inc(s_w["alibi"], 16)
            sp.wait_ge(s_end["xattn1"], 1)
            load(awv1, "av1", KD, s_w["av1"])
            load(awo1, "ao1", KD, s_w["ao1"])
            for e in range(EXPERTS1):
                sp.dma_start(wexp1[:, e * W1:(e + 1) * W1], t["experts1"][e * P:(e + 1) * P, :]).then_inc(s_w["experts1"], 16)
            sp.wait_ge(s_end["attn1"], 1)
            load(router1, "router1", KD, s_w["tables1"])
            load_row(brouter, "brouter1", s_w["tables1"])
            load_row(iota8, "iota8", s_w["tables1"])
            sp.dma_start(bexp[0:EXPERTS1, :], t["bexp1"]).then_inc(s_w["tables1"], 16)
            with sp.Fori(0, TILES) as i:
                sp.wait_ge(s_final, i + 1)
                sp.dma_start(t["out"][bass.ds(i * P, P), :], x[:, bass.ds(i * D, D)]).then_inc(s_out, 16)
            sp.wait_ge(s_out, 16 * TILES)


def kernel(**inputs):
    import numpy as np
    from ml_dtypes import bfloat16 as bf16
    import concourse.bacc as bacc
    from concourse.bass_utils import run_bass_kernel_spmd

    a = {n: np.asarray(w) for n, w in inputs.items()}

    def transposed(w):
        return np.ascontiguousarray(np.swapaxes(w, -1, -2))

    ctx = a["ctx_1024"]
    ctxT = ctx.reshape(B, NCTX, KD, P).transpose(0, 3, 2, 1)
    token = np.arange(P)
    same = token[:, None] // S == token[None, :] // S
    seen = same & (token[:, None] >= token[None, :])
    mask_causal = np.where(seen, 0.0, np.where(same, MASKED, APART)).astype(np.float32)
    mask_apart = np.where(seen, 0.0, APART).astype(np.float32)
    qkv = a["L0_attn_w_qkv"].reshape(3, HD, D).transpose(0, 2, 1).reshape(3 * D, HD)
    arrays = {
        "x": a["x"].reshape(B * S, D),
        "ctx_head": ctxT[:, :, :, :S].reshape(TILES, SEQS, P, KD, S).transpose(0, 2, 3, 1, 4).reshape(TILES * P, D),
        "ctx_tail": ctxT[:, :, :, S:].reshape(B * P, KD * TAIL),
        "mask": np.repeat(a["mask_BxS2_bf0"][:, :S].reshape(TILES, SEQS, S).transpose(1, 0, 2),
                          S, axis=0).reshape(P, TILES * S),
        "q0": a["L0_xattn_Wq"], "k0": a["L0_xattn_Wk"], "v0": a["L0_xattn_Wv"], "o0": a["L0_xattn_Wo"],
        "bq0": a["L0_xattn_bq"], "bk0": a["L0_xattn_bk"], "bv0": a["L0_xattn_bv"], "bo0": a["L0_xattn_bo"],
        "qkv0": qkv, "gate0": transposed(a["L0_attn_w_gate"]), "out0": transposed(a["L0_attn_w_out"]),
        "ident": np.eye(P, dtype=np.float32), "mask_causal": mask_causal, "mask_apart": mask_apart,
    }
    def by_partition(w):
        n, rows, cols = w.shape
        return w.reshape(n, rows // P, P, cols).transpose(0, 2, 1, 3).reshape(n * P, rows // P * cols)

    dk = D // H
    inv_freq = (1.0 / 10000.0 ** (np.arange(0, dk, 2, dtype=np.float32) / dk)).astype(np.float32)
    freqs = (token % S).astype(np.float32)[:, None] * inv_freq[None, :]
    cos, sin = (np.tile(np.repeat(f(freqs), 2, axis=-1), (1, H)).astype(np.float32) for f in (np.cos, np.sin))
    sin = sin * np.tile(np.array([-1, 1], np.float32), D // 2)
    scale = np.float32(dk ** -0.5)
    places = Attention("attn1", dk, {}).places
    slopes = 2.0 ** (-8.0 * np.array(places, dtype=np.float32) / H)
    rel = -np.abs(token[:, None] - token[None, :]).astype(np.float32)
    alibi = np.where(same[:, None, :], slopes[None, :, None].astype(np.float32) * rel[:, None, :], APART)
    arrays.update({
        "experts0": np.concatenate([by_partition(transposed(a["L0_ffn_" + n])) for n in ("w_gate", "w_up", "w_down")], axis=1),
        "router0": transposed(a["L0_ffn_gate_w"]),
        "iota64": np.tile(np.arange(EXPERTS, dtype=np.float32), (P, 1)),
        "iota128": np.tile(np.arange(CAP, dtype=np.float32), (P, 1)),
        "tokens": np.stack([np.stack([token, np.full(P, j), np.ones(P)], -1) for j in range(TILES)], 1)
        .reshape(P, TILES * 3).astype(np.float32),
        "tri": (token[:, None] < token[None, :]).astype(bf16), "ones": np.ones((P, P), bf16),
        "q1": transposed(a["L1_xattn_Wq"]), "k1": a["L1_xattn_Wk"], "v1": transposed(a["L1_xattn_Wv"]),
        "o1": transposed(a["L1_xattn_Wo"]),
        "bq1": a["L1_xattn_bq"], "bk1": a["L1_xattn_bk"], "bv1": a["L1_xattn_bv"], "bo1": a["L1_xattn_bo"],
        "ctx_last": ctxT[:, :, :, -1].transpose(1, 2, 0).reshape(P, KD * B),
        "ctx": ctx, "ctxT": ctxT.reshape(B * P, KD * NCTX),
        "aq1": transposed(a["L1_attn_Wq"]), "ak1": transposed(a["L1_attn_Wk"]), "av1": transposed(a["L1_attn_Wv"]),
        "ao1": transposed(a["L1_attn_Wo"]),
        "rope": np.concatenate([cos * scale, sin * scale, cos, sin], axis=1).astype(np.float32),
        "alibi": alibi.reshape(P, H * P).astype(np.float32),
        "experts1": by_partition(transposed(a["L1_ffn_W_experts"])),
        "router1": transposed(a["L1_ffn_W_router"]), "brouter1": a["L1_ffn_b_router"], "bexp1": a["L1_ffn_b_experts"],
        "iota8": np.arange(EXPERTS1, dtype=np.float32),
    })
    nc = bacc.Bacc("TRN2", target_bir_lowering=False, num_devices=1)
    arrays = {"in_" + n: np.ascontiguousarray(w) for n, w in arrays.items()}
    t = {n[3:]: nc.dram_tensor(n, w.shape, mybir.dt.from_np(w.dtype), kind="ExternalInput").ap()
         for n, w in arrays.items()}
    t["out"] = nc.dram_tensor("out", (B * S, D), F32, kind="ExternalOutput").ap()
    build(nc, t)
    r = run_bass_kernel_spmd(nc, [arrays], core_ids=[0])
    return r.results[0]["out"].reshape(B, S, D)
```
